# Optimizing a Trainium2 kernel written in Bass

```python
import numpy as np
import jax
import jax.numpy as jnp

def _softmax(x, axis=-1):
    return jax.nn.softmax(x, axis=axis)

def _gelu(x):
    return jax.nn.gelu(x, approximate=True)

def _silu(x):
    return jax.nn.silu(x)

def _sigmoid(x):
    return jax.nn.sigmoid(x)

def _layernorm(x, axis=-1, eps=1e-05):
    m = jnp.mean(x, axis=axis, keepdims=True)
    v = jnp.var(x, axis=axis, keepdims=True)
    return (x - m) / jnp.sqrt(v + eps)

def _scatter_add(tgt, idx, src, axis=0):
    return tgt.at[idx].add(src)

def _segment_sum(src, seg, n):
    return jax.ops.segment_sum(src, seg, n)
kernel_name = 'mk_xattn_ffn_d1_seqx_r4_89e812'

def setup_inputs(seed: int=0):
    np.random.seed(seed)
    _w = jnp.asarray

    def _rec_inputs():
        import jax
        import jax.numpy as jnp
        _rk = jax.random.key(seed)
        x = 0.5 + 0.2887 * jax.random.normal(jax.random.fold_in(_rk, 1), (4, 512, 512), jnp.float32)
        _lenS = 512 - jax.random.randint(jax.random.fold_in(_rk, 7), (4,), 0, max(1, 512 // 4) + 1, jnp.int32)
        _lenS2 = 512 - jax.random.randint(jax.random.fold_in(_rk, 8), (4,), 0, max(1, 512 // 4) + 1, jnp.int32)
        _ctx_512P = jax.random.normal(jax.random.fold_in(_rk, 11), (4, 16, 128), jnp.float32)
        _ctx_512c = jax.random.dirichlet(jax.random.fold_in(_rk, 511), 0.3 * jnp.ones((16,), jnp.float32), (4, 512))
        _ctx_512t = jnp.einsum('bsk,bkd->bsd', _ctx_512c, _ctx_512P)
        _ctx_512t = _ctx_512t * jax.lax.rsqrt(jnp.mean(jnp.square(_ctx_512t)) + 1e-12) * 0.953939
        ctx_512 = -0.000392918 + 0.999932 * (_ctx_512t + 0.3 * jax.random.normal(jax.random.fold_in(_rk, 611), (4, 512, 128), jnp.float32))
        return (x, ctx_512)
    x, ctx_512 = _rec_inputs()

    def _L0_xattn_setup():
        import jax, jax.numpy as jnp
        import numpy as np
        B, N, D = (16, 512, 128)
        H = 4
        TOP_K_RATIO = 0.3
        key = jax.random.key(seed)
        k1, k2, k3, k4 = jax.random.split(key, 4)
        h = jax.random.normal(k1, (B, N, D), dtype=jnp.float32)
        adj_raw = jax.random.uniform(k2, (B, N, N), dtype=jnp.float32)
        lim = 1.0 / np.sqrt(D)
        Wq = jax.random.uniform(k3, (D, D), minval=-lim, maxval=lim, dtype=jnp.float32)
        Wk = jax.random.uniform(k4, (D, D), minval=-lim, maxval=lim, dtype=jnp.float32)
        gamma_raw = jnp.float32(-0.85)
        return {'h': h, 'adj_raw': adj_raw, 'Wq': Wq, 'Wk': Wk, 'gamma_raw': gamma_raw}
    _L0_xattn_all = _L0_xattn_setup()
    _L0_xattn_in = {k: v for k, v in _L0_xattn_all.items() if k in ('Wq', 'Wk', 'gamma_raw')}
    del _L0_xattn_all

    def _L0_ffn_setup():
        import jax, jax.numpy as jnp
        import numpy as np
        B, S, H = (2, 512, 512)
        E, G, TKG, K = (32, 8, 4, 8)
        I, SI = (256, 512)
        ROUTED_SCALE = 2.5

        def _moe_forward(hidden_states, router_w, router_bias, w_gate, w_up, w_down, sw_gate, sw_up, sw_down):
            x = hidden_states.reshape(-1, H)
            T = x.shape[0]
            logits = x.astype(jnp.float32) @ router_w.astype(jnp.float32)
            scores = jax.nn.sigmoid(logits)
            scores_grouped = (scores + router_bias).reshape(T, G, E // G)
            top2, _ = jax.lax.top_k(scores_grouped, 2)
            group_scores = top2.sum(-1)
            _, top_groups = jax.lax.top_k(group_scores, TKG)
            mask = jnp.ones((T, G), bool).at[jnp.arange(T)[:, None], top_groups].set(False)
            masked = jnp.where(mask[:, :, None], 0.0, scores_grouped).reshape(T, E)
            _, top_k_index = jax.lax.top_k(masked, K)
            tkw = jnp.take_along_axis(scores, top_k_index, axis=-1)
            tkw = tkw / tkw.sum(-1, keepdims=True)
            tkw = (tkw * ROUTED_SCALE).astype(hidden_states.dtype)
            flat_idx = top_k_index.reshape(-1)
            sort_idx = jnp.argsort(flat_idx)
            xs = jnp.repeat(x, K, axis=0)[sort_idx]
            group_sizes = jnp.bincount(flat_idx, length=E).astype(jnp.int32)
            gate = jax.lax.ragged_dot(xs, w_gate, group_sizes)
            up = jax.lax.ragged_dot(xs, w_up, group_sizes)
            down = jax.lax.ragged_dot(jax.nn.silu(gate) * up, w_down, group_sizes)
            unsort = jnp.argsort(sort_idx)
            routed = (down[unsort].reshape(T, K, H) * tkw[..., None]).sum(axis=1)
            shared = jax.nn.silu(x @ sw_gate) * (x @ sw_up) @ sw_down
            return (routed + shared).reshape(hidden_states.shape)
        key = jax.random.key(seed)
        ks = jax.random.split(key, 9)

        def w(k, shape, fan_in):
            return jax.random.normal(k, shape, jnp.float32) / np.float32(np.sqrt(fan_in))
        return dict(hidden_states=jax.random.normal(ks[0], (B, S, H), jnp.float32), router_w=w(ks[1], (H, E), H), router_bias=jnp.zeros((E,), jnp.float32), w_gate=w(ks[2], (E, H, I), H), w_up=w(ks[3], (E, H, I), H), w_down=w(ks[4], (E, I, H), I), sw_gate=w(ks[5], (H, SI), H), sw_up=w(ks[6], (H, SI), H), sw_down=w(ks[7], (SI, H), SI))
    _L0_ffn_all = _L0_ffn_setup()
    _L0_ffn_in = {k: v for k, v in _L0_ffn_all.items() if k in ('router_w', 'router_bias', 'w_gate', 'w_up', 'w_down', 'sw_gate', 'sw_up', 'sw_down')}
    del _L0_ffn_all
    return {'x': x, 'ctx_512': ctx_512, 'L0_xattn_Wq': _L0_xattn_in['Wq'], 'L0_xattn_Wk': _L0_xattn_in['Wk'], 'L0_xattn_gamma_raw': _L0_xattn_in['gamma_raw'], 'L0_ffn_router_w': _L0_ffn_in['router_w'], 'L0_ffn_router_bias': _L0_ffn_in['router_bias'], 'L0_ffn_w_gate': _L0_ffn_in['w_gate'], 'L0_ffn_w_up': _L0_ffn_in['w_up'], 'L0_ffn_w_down': _L0_ffn_in['w_down'], 'L0_ffn_sw_gate': _L0_ffn_in['sw_gate'], 'L0_ffn_sw_up': _L0_ffn_in['sw_up'], 'L0_ffn_sw_down': _L0_ffn_in['sw_down']}

def reference(x, ctx_512, L0_xattn_Wq, L0_xattn_Wk, L0_xattn_gamma_raw, L0_ffn_router_w, L0_ffn_router_bias, L0_ffn_w_gate, L0_ffn_w_up, L0_ffn_w_down, L0_ffn_sw_gate, L0_ffn_sw_up, L0_ffn_sw_down):
    import jax
    import jax.numpy as jnp

    def _L0_xattn_ref(h, adj_raw, Wq, Wk, gamma_raw):
        import jax, jax.numpy as jnp
        import numpy as np
        B, N, D = (16, 512, 128)
        H = 4
        TOP_K_RATIO = 0.3
        b, n, dm = h.shape
        d = dm // H
        Q = (h @ Wq.T).reshape(b, n, H, d).transpose(0, 2, 1, 3)
        K = (h @ Wk.T).reshape(b, n, H, d).transpose(0, 2, 1, 3)
        sim = jnp.einsum('bhnd,bhmd->bnm', Q, K) / (jnp.sqrt(jnp.float32(d)) * H)
        k = max(1, int(n * TOP_K_RATIO))
        topk_vals = jax.lax.top_k(sim, k)[0]
        threshold = topk_vals[:, :, -1:]
        sparse_mask = (sim >= threshold).astype(sim.dtype)
        A_learned = jax.nn.sigmoid(sim) * sparse_mask
        A_learned = (A_learned + jnp.swapaxes(A_learned, -1, -2)) * 0.5
        gamma = jax.nn.sigmoid(gamma_raw)
        return (1.0 - gamma) * adj_raw + gamma * A_learned

    def _L0_ffn_ref(hidden_states, router_w, router_bias, w_gate, w_up, w_down, sw_gate, sw_up, sw_down):
        import jax, jax.numpy as jnp
        import numpy as np
        B, S, H = (2, 512, 512)
        E, G, TKG, K = (32, 8, 4, 8)
        I, SI = (256, 512)
        ROUTED_SCALE = 2.5

        def _moe_forward(hidden_states, router_w, router_bias, w_gate, w_up, w_down, sw_gate, sw_up, sw_down):
            x = hidden_states.reshape(-1, H)
            T = x.shape[0]
            logits = x.astype(jnp.float32) @ router_w.astype(jnp.float32)
            scores = jax.nn.sigmoid(logits)
            scores_grouped = (scores + router_bias).reshape(T, G, E // G)
            top2, _ = jax.lax.top_k(scores_grouped, 2)
            group_scores = top2.sum(-1)
            _, top_groups = jax.lax.top_k(group_scores, TKG)
            mask = jnp.ones((T, G), bool).at[jnp.arange(T)[:, None], top_groups].set(False)
            masked = jnp.where(mask[:, :, None], 0.0, scores_grouped).reshape(T, E)
            _, top_k_index = jax.lax.top_k(masked, K)
            tkw = jnp.take_along_axis(scores, top_k_index, axis=-1)
            tkw = tkw / tkw.sum(-1, keepdims=True)
            tkw = (tkw * ROUTED_SCALE).astype(hidden_states.dtype)
            flat_idx = top_k_index.reshape(-1)
            sort_idx = jnp.argsort(flat_idx)
            xs = jnp.repeat(x, K, axis=0)[sort_idx]
            group_sizes = jnp.bincount(flat_idx, length=E).astype(jnp.int32)
            gate = jax.lax.ragged_dot(xs, w_gate, group_sizes)
            up = jax.lax.ragged_dot(xs, w_up, group_sizes)
            down = jax.lax.ragged_dot(jax.nn.silu(gate) * up, w_down, group_sizes)
            unsort = jnp.argsort(sort_idx)
            routed = (down[unsort].reshape(T, K, H) * tkw[..., None]).sum(axis=1)
            shared = jax.nn.silu(x @ sw_gate) * (x @ sw_up) @ sw_down
            return (routed + shared).reshape(hidden_states.shape)
        return _moe_forward(hidden_states, router_w, router_bias, w_gate, w_up, w_down, sw_gate, sw_up, sw_down)
    x = x + _L0_xattn_ref(ctx_512, _layernorm(x, axis=-1), L0_xattn_Wq, L0_xattn_Wk, L0_xattn_gamma_raw)
    x = x + _L0_ffn_ref(_layernorm(x, axis=-1), L0_ffn_router_w, L0_ffn_router_bias, L0_ffn_w_gate, L0_ffn_w_up, L0_ffn_w_down, L0_ffn_sw_gate, L0_ffn_sw_up, L0_ffn_sw_down)
    return x

_drawn_inputs = setup_inputs


def setup_inputs(seed=0):
    import zlib

    import numpy as np

    out = dict(_drawn_inputs(seed))
    spreads = {'L0_ffn_router_bias': (0.0, 0.1)}
    factors = {}
    for name, (base, spread) in spreads.items():
        noise = np.random.default_rng([zlib.crc32(name.encode()), seed]).standard_normal(out[name].shape)
        drawn = base * np.exp(spread * noise) if base else spread * noise
        out[name] = jnp.asarray(drawn.astype(out[name].dtype))
    for name, factor in factors.items():
        out[name] = (out[name] * factor).astype(out[name].dtype)
    return out
```

```python
from contextlib import ExitStack

import numpy as np

import concourse.bass as bass
from concourse import mybir

F32 = mybir.dt.float32
F16 = mybir.dt.float16
ALU = mybir.AluOpType
ACT = mybir.ActivationFunctionType
AX = mybir.AxisListType

P = 128
HEADS = 4
TOP_K_RATIO = 0.3
EPS = 1e-5
GROUPS, TOP_GROUPS, TOP_EXPERTS = 8, 4, 8
ROUTED_SCALE = 2.5
BISECTIONS = 26
LOWEST = -3.0e38
W_SCALE = 256.0


class Chain:

    def __init__(self, engine, sem, base=0):
        self.engine, self.sem, self.base, self.n = engine, sem, base, 0

    def done(self, instruction):
        self.n += 1
        instruction.then_inc(self.sem, 1)

    def settle(self):
        self.engine.wait_ge(self.sem, self.base + self.n)

    def step(self, instruction):
        self.done(instruction)
        self.settle()


def xattn_moe_kernel(nc, x, ctx_in, Wq, Wk, gamma_raw, router_w, router_bias, w_gate, w_up, w_down,
                     sw_gate, sw_up, sw_down, out):
    B, N, H = x.shape
    D = ctx_in.shape[2]
    E, _, I = w_gate.shape
    SI = sw_gate.shape[1]
    RT = N // P
    KC = H // P
    IC = I // P
    TT = B * RT
    EX = E + SI // I
    EG = E // GROUPS
    KEEP = max(1, int(N * TOP_K_RATIO))
    SIM_SCALE = 1.0 / (float(np.sqrt(np.float32(D // HEADS))) * HEADS)
    assert D == P and N == 512 and H == 512 and IC == 2

    with ExitStack() as stack:
        def sb(name, shape, dt=F32):
            return stack.enter_context(nc.sbuf_tensor(name, shape, dt))

        def sem(name):
            return stack.enter_context(nc.semaphore(name))

        bank = [stack.enter_context(nc.psum_tensor(f"bank{i}", [P, 512], F32)) for i in range(8)]

        xT16 = sb("xT16", [P, 2, KC, TT * P], F16)
        route = sb("route", [P, TT, EX])
        acc = sb("acc", [P, TT, H])
        ident = sb("ident", [P, P])
        w_qk = sb("w_qk", [P, 2, D])
        w_qkT = sb("w_qkT", [P, 2, D])
        gcol = sb("gcol", [P, 4])
        rw = sb("rw", [P, KC, E])
        bias = sb("bias", [P, E])
        ctx_sb = sb("ctx_sb", [P, RT, D])
        x_sb = sb("x_sb", [P, RT, H])
        base = sb("base", [P, RT, H])
        hT = sb("hT", [P, N])
        qT = sb("qT", [P, N])
        kT = sb("kT", [P, N])
        sim = sb("sim", [P, RT, N])
        adj = sb("adj", [P, RT, N])
        junk = sb("junk", [P, RT, N], mybir.dt.bfloat16)
        tmp = sb("tmp", [P, N])
        xn = sb("xn", [P, RT, H])
        xT32 = sb("xT32", [P, RT, KC, P])
        st6 = sb("st6", [P, RT, 6])
        mv = sb("mv", [P, RT, 2])
        ve = sb("ve", [P, RT])
        sd = sb("sd", [P, RT])
        rs = sb("rs", [P, RT])
        nt = sb("nt", [P, RT])
        nt2 = sb("nt2", [P, RT])
        coefA = sb("coefA", [P, RT])
        coefB = sb("coefB", [P, RT])
        mx = sb("mx", [P, RT])
        rng = sb("rng", [P, RT])
        lo = sb("lo", [P, RT])
        mid = sb("mid", [P, RT])
        cnt = sb("cnt", [P, RT])
        dlt = sb("dlt", [P, RT])
        scores = sb("scores", [P, RT, E])
        sg = sb("sg", [P, RT, E])
        pmx = sb("pmx", [P, RT, GROUPS, 2])
        pmn = sb("pmn", [P, RT, GROUPS, 2])
        t1 = sb("t1", [P, RT, GROUPS])
        t2 = sb("t2", [P, RT, GROUPS])
        t3 = sb("t3", [P, RT, GROUPS])
        gs = sb("gs", [P, RT, GROUPS + TOP_GROUPS])
        g8 = sb("g8", [P, RT, 8])
        gtaken = sb("gtaken", [P, RT, GROUPS + TOP_GROUPS])
        gkeep = sb("gkeep", [P, RT, GROUPS])
        masked = sb("masked", [P, RT, E])
        e8 = sb("e8", [P, RT, 8])
        etaken = sb("etaken", [P, RT, E])
        wsel = sb("wsel", [P, RT, E])
        wsum = sb("wsum", [P, RT])
        stage_gu = sb("stage_gu", [P, 2, KC, 2, I])
        stage_dn = sb("stage_dn", [P, 2, IC, H])
        gu16 = sb("gu16", [P, 2, 2, KC, 2 * I], F16)
        dn16 = sb("dn16", [P, 2, 2, IC, H], F16)
        silu = sb("silu", [P, 2, I])
        hid = sb("hid", [P, 2, I])
        hT16 = sb("hT16", [P, 2, 2, I], F16)

        names = ("consts ident_zero small_loaded ctx_loaded x_loaded wT_ready wT_copied ctxT_ready hT_ready "
                 "qk_ready qk_copied sim_ready sim_copied dve_chain act_chain pool_chain gamma_ready var_ready sqrt_ready "
                 "coef_ready base_ready sig_ready adj_ready adjT_ready adjT_used xn_ready xnT_ready xT32_ready "
                 "xhi_ready xlo_ready logits_ready scores_ready routed wload0 wload1 whi_ready wlo_ready gu_ready "
                 "silu_ready hid_ready hidT_ready hhi_ready hlo_ready down_ready added stored").split()
        S = {n: sem(n) for n in names}

        def _sl(b, i):
            return bass.ds(b * (RT * P) + i * P, P)

        with nc.Block() as block:
            @block.sync
            def _(sp):
                for i, w in enumerate((Wq, Wk)):
                    sp.dma_start(w_qk[:, i, :], w).then_inc(S["small_loaded"], 16)
                sp.dma_start(gcol[:, 0:1], gamma_raw.partition_broadcast(P)).then_inc(S["small_loaded"], 16)
                sp.dma_start(rw[:, :, :], router_w.rearrange("(k p) e -> p k e", p=P)).then_inc(S["small_loaded"], 16)
                sp.dma_start(bias[:, :], router_bias.partition_broadcast(P)).then_inc(S["small_loaded"], 16)
                for b in range(B):
                    sp.wait_ge(S["ctxT_ready"], b)
                    sp.dma_start(ctx_sb[:, :, :], ctx_in.rearrange("b (i p) d -> b p i d", p=P)[bass.ds(b, 1)].rearrange("b p i d -> (b p) i d")).then_inc(S["ctx_loaded"], 16)
                    sp.wait_ge(S["base_ready"], b * RT)
                    sp.dma_start(x_sb[:, :, :], x.rearrange("b (i p) h -> b p i h", p=P)[bass.ds(b, 1)].rearrange("b p i h -> (b p) i h")).then_inc(S["x_loaded"], 16)

            @block.gpsimd
            def _(pool):
                nc.gpsimd.memset(ident[:, :], 0.0).then_inc(S["ident_zero"], 1)
                pool.wait_ge(S["ident_zero"], 1)
                nc.gpsimd.affine_select(out=ident[:, :], in_=ident[:, :], compare_op=ALU.not_equal, fill=1.0,
                                        base=0, pattern=[[-1, P]], channel_multiplier=1).then_inc(S["consts"], 1)
                nc.gpsimd.memset(route[:, :, E:EX], 1.0).then_inc(S["consts"], 1)
                nc.gpsimd.memset(gs[:, :, GROUPS:], LOWEST).then_inc(S["consts"], 1)
                for b in range(B):
                    pool.wait_ge(S["coef_ready"], b + 1)
                    pool.wait_ge(S["x_loaded"], b * 16 + 16)
                    pool.wait_ge(S["xn_ready"], b)
                    for i in range(RT):
                        nc.gpsimd.tensor_scalar(base[:, i, :], x_sb[:, i, :], coefA[:, i:i + 1], coefB[:, i:i + 1],
                                                ALU.mult, ALU.add).then_inc(S["base_ready"], 1)

            @block.tensor
            def _(pe):
                pe.wait_ge(S["consts"], 1)
                pe.wait_ge(S["small_loaded"], 5 * 16)
                for i in range(2):
                    nc.tensor.transpose(bank[1][:, i * D:(i + 1) * D], w_qk[:, i, :], ident[:, :]).then_inc(S["wT_ready"], 1)
                pe.wait_ge(S["wT_copied"], 1)
                for b in range(B):
                    pe.wait_ge(S["ctx_loaded"], b * 16 + 16)
                    for i in range(RT):
                        t = nc.tensor.transpose(bank[0][:, i * P:(i + 1) * P], ctx_sb[:, i, :], ident[:, :])
                    t.then_inc(S["ctxT_ready"], 1)
                    pe.wait_ge(S["hT_ready"], b + 1)
                    for i in range(2):
                        nc.tensor.matmul(bank[1 + i][:, :], w_qkT[:, i, :], hT[:, :], start=True, stop=True).then_inc(S["qk_ready"], 1)
                    pe.wait_ge(S["qk_copied"], 2 * b + 2)
                    for i in range(RT):
                        nc.tensor.matmul(bank[3 + i][:, :], qT[:, i * P:(i + 1) * P], kT[:, :], start=True, stop=True).then_inc(S["sim_ready"], 1)
                    pe.wait_ge(S["adj_ready"], RT * b + RT)
                    pe.wait_ge(S["sim_copied"], RT * b + RT)
                    for i in range(RT):
                        for j in range(RT):
                            t = nc.tensor.transpose(bank[3 + i][:, j * P:(j + 1) * P], adj[:, j, i * P:(i + 1) * P], ident[:, :])
                        t.then_inc(S["adjT_ready"], 1)
                    pe.wait_ge(S["xn_ready"], b + 1)
                    for i in range(RT):
                        if i >= 2:
                            pe.wait_ge(S["xlo_ready"], RT * b + i - 1)
                        for k in range(KC):
                            t = nc.tensor.transpose(bank[1 + i % 2][:, k * P:(k + 1) * P], xn[:, i, k * P:(k + 1) * P], ident[:, :])
                        t.then_inc(S["xnT_ready"], 1)
                    for i in range(RT):
                        pe.wait_ge(S["xT32_ready"], RT * b + i + 1)
                        for k in range(KC):
                            t = nc.tensor.matmul(bank[7][:, i * E:(i + 1) * E], xT32[:, i, k, :], rw[:, k, :],
                                                 start=(k == 0), stop=(k == KC - 1))
                    t.then_inc(S["logits_ready"], 1)
                    pe.wait_ge(S["scores_ready"], b + 1)

            @block.scalar
            def _(act):
                act.wait_ge(S["small_loaded"], 5 * 16)
                nc.scalar.activation(gcol[:, 1:2], gcol[:, 0:1], ACT.Sigmoid).then_inc(S["gamma_ready"], 1)
                for b in range(B):
                    act.wait_ge(S["var_ready"], 2 * b + 1)
                    nc.scalar.activation(sd[:, :], ve[:, :], ACT.Sqrt).then_inc(S["sqrt_ready"], 1)
                    act.wait_ge(S["qk_ready"], 2 * b + 2)
                    nc.scalar.copy(kT[:, :], bank[2][:, :]).then_inc(S["qk_copied"], 1)
                    act.wait_ge(S["adj_ready"], RT * b)
                    act.wait_ge(S["adjT_ready"], RT * b)
                    act.wait_ge(S["adjT_used"], RT * b)
                    for i in range(RT):
                        act.wait_ge(S["sim_ready"], RT * b + i + 1)
                        nc.scalar.mul(sim[:, i, :], bank[3 + i][:, :], SIM_SCALE).then_inc(S["sim_copied"], 1)
                    act.wait_ge(S["sim_copied"], RT * b + RT)
                    nc.scalar.activation(adj[:, :, :], sim[:, :, :], ACT.Sigmoid).then_inc(S["sig_ready"], 1)
                    act.wait_ge(S["var_ready"], 2 * b + 2)
                    nc.scalar.activation(sd[:, :], ve[:, :], ACT.Sqrt).then_inc(S["sqrt_ready"], 1)
                    for i in range(RT):
                        act.wait_ge(S["xnT_ready"], RT * b + i + 1)
                        act.wait_ge(S["xT32_ready"], RT * b + i + 1)
                        nc.scalar.copy(xT16[:, 0, :, _sl(b, i)],
                                       xT32[:, i, :, :]).then_inc(S["xhi_ready"], 1)
                    act.wait_ge(S["logits_ready"], b + 1)
                    nc.scalar.activation(scores[:, :, :], bank[7][:, 0:RT * E].rearrange("p (i e) -> p i e", e=E),
                                         ACT.Sigmoid).then_inc(S["scores_ready"], 1)

            @block.vector
            def _(dve):
                for i in range(2):
                    pass
                dve.wait_ge(S["wT_ready"], 2)
                nc.vector.tensor_copy(w_qkT[:, :, :], bank[1][:, 0:2 * D].rearrange("p (a d) -> p a d", a=2)).then_inc(S["wT_copied"], 1)
                dve.wait_ge(S["gamma_ready"], 1)
                pre = Chain(dve, S["dve_chain"])
                pre.done(nc.vector.tensor_scalar(gcol[:, 2:3], gcol[:, 1:2], -1.0, 1.0, ALU.mult, ALU.add))
                pre.step(nc.vector.tensor_scalar(gcol[:, 3:4], gcol[:, 1:2], 0.5, None, ALU.mult))
                dve.wait_ge(S["consts"], 3)

                def batch(b, per_batch):
                    v = nc.vector
                    ch = Chain(dve, S["dve_chain"], b * per_batch + pre.n)

                    def inverse_std(nth):
                        for i in range(RT):
                            ch.done(v.bn_aggr(mv[:, i, :], st6[:, i, :]))
                        ch.settle()
                        v.tensor_scalar(ve[:, :], mv[:, :, 1], EPS, None, ALU.add).then_inc(S["var_ready"], 1)
                        dve.wait_ge(S["sqrt_ready"], 2 * b + nth)
                        ch.step(v.reciprocal(rs[:, :], sd[:, :]))
                        ch.step(v.tensor_tensor(nt[:, :], rs[:, :], rs[:, :], ALU.mult))
                        ch.step(v.tensor_tensor(nt2[:, :], nt[:, :], ve[:, :], ALU.mult))
                        ch.step(v.tensor_scalar(nt[:, :], nt2[:, :], -0.5, 1.5, ALU.mult, ALU.add))
                        ch.step(v.tensor_tensor(rs[:, :], rs[:, :], nt[:, :], ALU.mult))

                    dve.wait_ge(S["ctxT_ready"], b + 1)
                    v.tensor_copy(hT[:, :], bank[0][:, :]).then_inc(S["hT_ready"], 1)
                    dve.wait_ge(S["x_loaded"], b * 16 + 16)
                    for i in range(RT):
                        ch.done(v.bn_stats(st6[:, i, :], x_sb[:, i, :]))
                    ch.settle()
                    dve.wait_ge(S["qk_ready"], 2 * b + 2)
                    v.tensor_copy(qT[:, :], bank[1][:, :]).then_inc(S["qk_copied"], 1)
                    inverse_std(1)
                    ch.step(v.tensor_scalar(nt[:, :], rs[:, :], gcol[:, 2:3], None, ALU.mult))
                    ch.done(v.tensor_scalar(coefA[:, :], nt[:, :], 1.0, None, ALU.add))
                    v.scalar_tensor_tensor(coefB[:, :], nt[:, :], -1.0, mv[:, :, 0], ALU.mult, ALU.mult).then_inc(S["coef_ready"], 1)

                    dve.wait_ge(S["sim_copied"], RT * b + RT)
                    ch.done(v.tensor_reduce(mx[:, :], sim[:, :, :], AX.X, ALU.max))
                    ch.step(v.tensor_reduce(lo[:, :], sim[:, :, :], AX.X, ALU.min))
                    ch.step(v.tensor_tensor(rng[:, :], mx[:, :], lo[:, :], ALU.subtract))
                    ch.step(v.tensor_scalar(rng[:, :], rng[:, :], 0.5, None, ALU.mult))
                    per = RT + 4
                    before = ch.n
                    with dve.Fori(0, BISECTIONS) as it:
                        inner = Chain(dve, S["dve_chain"], b * per_batch + it * per + (pre.n + before))
                        inner.step(v.tensor_tensor(mid[:, :], lo[:, :], rng[:, :], ALU.add))
                        for i in range(RT):
                            inner.done(v.tensor_scalar(junk[:, i, :], sim[:, i, :], mid[:, i:i + 1], 0.0, ALU.is_ge, ALU.add,
                                                       accum_out=cnt[:, i:i + 1]))
                        inner.settle()
                        inner.step(v.scalar_tensor_tensor(dlt[:, :], cnt[:, :], KEEP - 0.5, rng[:, :], ALU.is_ge, ALU.mult))
                        inner.done(v.tensor_tensor(lo[:, :], lo[:, :], dlt[:, :], ALU.add))
                        inner.step(v.tensor_scalar(rng[:, :], rng[:, :], 0.5, None, ALU.mult))
                        assert inner.n == per
                    ch.n = before + per * BISECTIONS

                    dve.wait_ge(S["sig_ready"], b + 1)
                    for i in range(RT):
                        v.scalar_tensor_tensor(adj[:, i, :], sim[:, i, :], lo[:, i:i + 1], adj[:, i, :],
                                               ALU.is_ge, ALU.mult).then_inc(S["adj_ready"], 1)
                    dve.wait_ge(S["adj_ready"], RT * b + RT)
                    dve.wait_ge(S["base_ready"], RT * b + RT)
                    for i in range(RT):
                        dve.wait_ge(S["adjT_ready"], RT * b + i + 1)
                        v.tensor_tensor(tmp[:, :], adj[:, i, :], bank[3 + i][:, :], ALU.add).then_inc(S["adjT_used"], 1)
                        dve.wait_ge(S["adjT_used"], RT * b + i + 1)
                        ch.step(v.scalar_tensor_tensor(acc[:, bass.ds(b * RT + i, 1), :].rearrange("p a h -> p (a h)"), tmp[:, :], gcol[:, 3:4], base[:, i, :],
                                                       ALU.mult, ALU.add))
                        ch.done(v.bn_stats(st6[:, i, :], acc[:, bass.ds(b * RT + i, 1), :].rearrange("p a h -> p (a h)")))
                    ch.settle()
                    inverse_std(2)
                    for i in range(RT):
                        t = v.tensor_scalar(xn[:, i, :], acc[:, bass.ds(b * RT + i, 1), :].rearrange("p a h -> p (a h)"), mv[:, i, 0:1], rs[:, i:i + 1],
                                            ALU.subtract, ALU.mult)
                        if i < RT - 1:
                            ch.done(t)
                    t.then_inc(S["xn_ready"], 1)
                    for i in range(RT):
                        dve.wait_ge(S["xnT_ready"], RT * b + i + 1)
                        v.tensor_copy(xT32[:, i, :, :], bank[1 + i % 2][:, :].rearrange("p (k t) -> p k t", k=KC)).then_inc(S["xT32_ready"], 1)
                        dve.wait_ge(S["xhi_ready"], RT * b + i + 1)
                        v.tensor_tensor(xT16[:, 1, :, _sl(b, i)], xT32[:, i, :, :], xT16[:, 0, :, _sl(b, i)],
                                        ALU.subtract).then_inc(S["xlo_ready"], 1)

                    dve.wait_ge(S["scores_ready"], b + 1)
                    ch.step(v.tensor_tensor(sg[:, :, :], scores[:, :, :], bias[:, :].unsqueeze(1).to_broadcast([P, RT, E]), ALU.add))
                    q = sg[:, :, :].rearrange("p i (g a c) -> p i g a c", a=2, c=2)
                    for c in range(RT):
                        ch.done(v.tensor_tensor(pmx[:, c, :, :], q[:, c, :, :, 0], q[:, c, :, :, 1], ALU.max))
                        ch.done(v.tensor_tensor(pmn[:, c, :, :], q[:, c, :, :, 0], q[:, c, :, :, 1], ALU.min))
                    ch.settle()
                    ch.done(v.tensor_tensor(t1[:, :, :], pmx[:, :, :, 0], pmx[:, :, :, 1], ALU.max))
                    ch.done(v.tensor_tensor(t2[:, :, :], pmx[:, :, :, 0], pmx[:, :, :, 1], ALU.min))
                    ch.step(v.tensor_tensor(t3[:, :, :], pmn[:, :, :, 0], pmn[:, :, :, 1], ALU.max))
                    ch.step(v.tensor_tensor(t2[:, :, :], t2[:, :, :], t3[:, :, :], ALU.max))
                    ch.step(v.tensor_tensor(gs[:, :, 0:GROUPS], t1[:, :, :], t2[:, :, :], ALU.add))
                    for i in range(RT):
                        ch.done(v.max(g8[:, i, :], gs[:, i, 0:GROUPS]))
                    ch.settle()
                    ch.step(v.memset(g8[:, :, TOP_GROUPS:], LOWEST))
                    for i in range(RT):
                        ch.done(v.match_replace(gtaken[:, i, :], g8[:, i, :], gs[:, i, :], LOWEST))
                    ch.settle()
                    ch.step(v.tensor_scalar(gkeep[:, :, :], gtaken[:, :, 0:GROUPS], LOWEST / 2, None, ALU.is_le))
                    for i in range(RT):
                        ch.done(v.tensor_tensor(masked[:, i, :].rearrange("p (g c) -> p g c", c=EG), sg[:, i, :].rearrange("p (g c) -> p g c", c=EG),
                                                gkeep[:, i, :].unsqueeze(2).to_broadcast([P, GROUPS, EG]), ALU.mult))
                    ch.settle()
                    for i in range(RT):
                        ch.done(v.max(e8[:, i, :], masked[:, i, :]))
                    ch.settle()
                    for i in range(RT):
                        ch.done(v.match_replace(etaken[:, i, :], e8[:, i, :], masked[:, i, :], LOWEST))
                    ch.settle()
                    ch.step(v.scalar_tensor_tensor(wsel[:, :, :], etaken[:, :, :], LOWEST / 2, scores[:, :, :], ALU.is_le, ALU.mult))
                    ch.step(v.tensor_reduce(wsum[:, :], wsel[:, :, :], AX.X, ALU.add))
                    ch.step(v.reciprocal(wsum[:, :], wsum[:, :]))
                    for i in range(RT):
                        t = v.tensor_scalar(route[:, bass.ds(b * RT + i, 1), 0:E].rearrange("p a e -> p (a e)"), wsel[:, i, :], wsum[:, i:i + 1], ROUTED_SCALE, ALU.mult, ALU.mult)
                        if i < RT - 1:
                            ch.done(t)
                    t.then_inc(S["routed"], 1)
                    return ch.n

                PER_BATCH = 289
                for b in range(B):
                    n = batch(b, PER_BATCH)
                    assert n == PER_BATCH, n

        GU, HT, DN = (0, 1), (2, 3), (4, 5)

        with nc.Block() as block:
            def sources(e):
                if isinstance(e, int) and e >= E:
                    c = slice((e - E) * I, (e - E + 1) * I)
                    return sw_gate[:, c], sw_up[:, c], sw_down[c, :]
                return w_gate[e], w_up[e], w_down[e]

            def over_experts(engine, body):
                with engine.Fori(0, E - 1, 2) as e:
                    body(e, 0)
                    body(e + 1, 1)
                for e in range(E, EX):
                    body(e, e % 2)

            @block.sync
            def _(sp):
                def load(e, s):
                    if not isinstance(e, int) or e >= 2:
                        sp.wait_ge(S["wlo_ready"], 2 * e - 2)
                    g, u, d = sources(e) if isinstance(e, int) else (None, None, None)
                    if g is None:
                        g, u, d = (w[bass.ds(e, 1)].rearrange("a k n -> (a k) n") for w in (w_gate, w_up, w_down))
                    sp.dma_start(stage_gu[:, s, :, 0, :], g.rearrange("(k p) i -> p k i", p=P)).then_inc(S[f"wload{s}"], 16)
                    sp.dma_start(stage_gu[:, s, :, 1, :], u.rearrange("(k p) i -> p k i", p=P)).then_inc(S[f"wload{s}"], 16)
                    sp.dma_start(stage_dn[:, s, :, :], d.rearrange("(k p) h -> p k h", p=P)).then_inc(S[f"wload{s}"], 16)

                load(0, 0)
                load(1, 1)
                with sp.Fori(2, E - 1, 2) as e:
                    load(e, 0)
                    load(e + 1, 1)
                for e in range(E, EX):
                    load(e, e % 2)

            def half(e, s):
                return (e - s) if isinstance(e, int) else (e - s)

            @block.scalar
            def _(act):
                def convert(e, s):
                    act.wait_ge(S[f"wload{s}"], (e - s) * 24 + 48)
                    nc.scalar.mul(gu16[:, s, 0, :, :], stage_gu[:, s, :, :, :].rearrange("p k a i -> p k (a i)"), W_SCALE).then_inc(S["whi_ready"], 1)
                    nc.scalar.mul(dn16[:, s, 0, :, :], stage_dn[:, s, :, :], W_SCALE).then_inc(S["whi_ready"], 1)

                def tile(n, s, first=False):
                    act.wait_ge(S["gu_ready"], n + 1)
                    if not first:
                        act.wait_ge(S["hid_ready"], n - 1)
                    nc.scalar.activation(silu[:, s, :], bank[GU[s]][:, 0:I], ACT.Silu, scale=1.0 / W_SCALE).then_inc(S["silu_ready"], 1)
                    act.wait_ge(S["hidT_ready"], n + 1)
                    if not first:
                        act.wait_ge(S["down_ready"], n - 1)
                    nc.scalar.copy(hT16[:, s, 0, :], bank[HT[s]][:, 0:I]).then_inc(S["hhi_ready"], 1)

                def body(e, s):
                    if isinstance(e, int) and e == 0:
                        convert(e, s)
                    else:
                        act.wait_ge(S["down_ready"], (e - 1) * TT)
                        convert(e, s)
                    if isinstance(e, int) and e == 0:
                        for n in range(2):
                            tile(n, n, first=True)
                        with act.Fori(2, TT - 1, 2) as g:
                            for s2 in range(2):
                                tile(g + s2, s2)
                    else:
                        with act.Fori(0, TT - 1, 2) as g:
                            for s2 in range(2):
                                tile(e * TT + g + s2, s2)
                body(0, 0)
                body(1, 1)
                with act.Fori(2, E - 1, 2) as e:
                    body(e, 0)
                    body(e + 1, 1)
                for e in range(E, EX):
                    body(e, e % 2)

            @block.vector
            def _(dve):
                def tile(e, g, s, first=False):
                    n = e * TT + g
                    v = nc.vector
                    dve.wait_ge(S["silu_ready"], n + 1)
                    if not first:
                        dve.wait_ge(S["hidT_ready"], n - 1)
                    v.scalar_tensor_tensor(hid[:, s, :], bank[GU[s]][:, I:2 * I], 1.0 / W_SCALE, silu[:, s, :],
                                           ALU.mult, ALU.mult).then_inc(S["hid_ready"], 1)
                    dve.wait_ge(S["hhi_ready"], n + 1)
                    v.tensor_tensor(hT16[:, s, 1, :], bank[HT[s]][:, 0:I], hT16[:, s, 0, :], ALU.subtract).then_inc(S["hlo_ready"], 1)
                    dve.wait_ge(S["down_ready"], n + 1)
                    a = acc[:, bass.ds(g, 1), :].rearrange("p a h -> p (a h)") if not isinstance(g, int) else acc[:, g, :]
                    r = route[:, bass.ds(g, 1), bass.ds(e, 1)].rearrange("p a e -> p (a e)") if not isinstance(g, int) or not isinstance(e, int) else route[:, g, e:e + 1]
                    v.scalar_tensor_tensor(a, bank[DN[s]][:, :], r, a, ALU.mult, ALU.add).then_inc(S["added"], 1)

                def body(e, s):
                    dve.wait_ge(S["whi_ready"], 2 * e + 2)
                    nc.vector.scalar_tensor_tensor(gu16[:, s, 1, :, :].rearrange("p k n -> p (k n)"), stage_gu[:, s, :, :, :].rearrange("p k a i -> p (k a i)"),
                                                   W_SCALE, gu16[:, s, 0, :, :].rearrange("p k n -> p (k n)"), ALU.mult, ALU.subtract).then_inc(S["wlo_ready"], 1)
                    nc.vector.scalar_tensor_tensor(dn16[:, s, 1, :, :].rearrange("p k n -> p (k n)"), stage_dn[:, s, :, :].rearrange("p k n -> p (k n)"),
                                                   W_SCALE, dn16[:, s, 0, :, :].rearrange("p k n -> p (k n)"), ALU.mult, ALU.subtract).then_inc(S["wlo_ready"], 1)
                    if isinstance(e, int) and e == 0:
                        for n in range(2):
                            tile(0, n, n, first=True)
                        with dve.Fori(2, TT - 1, 2) as g:
                            for s2 in range(2):
                                tile(0, g + s2, s2)
                    else:
                        with dve.Fori(0, TT - 1, 2) as g:
                            for s2 in range(2):
                                tile(e, g + s2, s2)
                scale = nc.vector.tensor_scalar(route[:, :, :], route[:, :, :], 1.0 / W_SCALE, None, ALU.mult)
                scale.then_inc(S["added"], 1)
                dve.wait_ge(S["added"], 1)
                body(0, 0)
                body(1, 1)
                with dve.Fori(2, E - 1, 2) as e:
                    body(e, 0)
                    body(e + 1, 1)
                for e in range(E, EX):
                    body(e, e % 2)

            @block.tensor
            def _(pe):
                def three(out_ap, stationary, moving, chunks):
                    parts = [(0, 0), (0, 1), (1, 0)]
                    for c in range(chunks):
                        for a, w in parts:
                            last = nc.tensor.matmul(out_ap, stationary(a, c), moving(w, c), start=(c == 0 and (a, w) == parts[0]),
                                                    stop=(c == chunks - 1 and (a, w) == parts[-1]))
                    return last

                def gate_up(n, g, s, ws):
                    cols = bass.ds(g * P, P)
                    three(bank[GU[s]][:, :], lambda a, c: xT16[:, a, c, cols], lambda w, c: gu16[:, ws, w, c, :], KC).then_inc(S["gu_ready"], 1)

                def transposes(n, s):
                    pe.wait_ge(S["hid_ready"], n + 1)
                    for c in range(IC):
                        t = nc.tensor.transpose(bank[HT[s]][:, c * P:(c + 1) * P], hid[:, s, c * P:(c + 1) * P], ident[:, :])
                    t.then_inc(S["hidT_ready"], 1)

                def down(n, s, ws):
                    pe.wait_ge(S["hlo_ready"], n + 1)
                    three(bank[DN[s]][:, :], lambda a, c: hT16[:, s, a, c * P:(c + 1) * P], lambda w, c: dn16[:, ws, w, c, :], IC).then_inc(S["down_ready"], 1)

                def body(e, ws):
                    pe.wait_ge(S["wlo_ready"], 2 * e + 2)
                    n0 = e * TT
                    if not (isinstance(e, int) and e == 0):
                        pe.wait_ge(S["hid_ready"], n0 - 1)
                    gate_up(n0, 0, 0, ws)
                    if not (isinstance(e, int) and e == 0):
                        pe.wait_ge(S["added"], n0)
                    transposes(n0, 0)
                    pe.wait_ge(S["hid_ready"], n0)
                    gate_up(n0 + 1, 1, 1, ws)
                    down(n0, 0, ws)
                    transposes(n0 + 1, 1)
                    with pe.Fori(2, TT - 1, 2) as g:
                        for s in range(2):
                            n = n0 + g + s
                            pe.wait_ge(S["hid_ready"], n - 1)
                            gate_up(n, g + s, s, ws)
                            pe.wait_ge(S["added"], n - 1)
                            down(n - 1, 1 - s, ws)
                            pe.wait_ge(S["hlo_ready"], n - 1)
                            transposes(n, s)
                    down(n0 + TT - 1, 1, ws)

                body(0, 0)
                body(1, 1)
                with pe.Fori(2, E - 1, 2) as e:
                    body(e, 0)
                    body(e + 1, 1)
                for e in range(E, EX):
                    body(e, e % 2)

        with nc.Block() as block:
            @block.sync
            def _(sp):
                sp.dma_start(out.rearrange("b (i p) h -> p (b i) h", p=P), acc[:, :, :]).then_inc(S["stored"], 16)
                sp.wait_ge(S["stored"], 16)


_INS = ["x", "ctx_512", "L0_xattn_Wq", "L0_xattn_Wk", "L0_xattn_gamma_raw", "L0_ffn_router_w", "L0_ffn_router_bias",
        "L0_ffn_w_gate", "L0_ffn_w_up", "L0_ffn_w_down", "L0_ffn_sw_gate", "L0_ffn_sw_up", "L0_ffn_sw_down"]
_OUTS = [((4, 512, 512), "float32")]


def kernel(**inputs):
    import numpy as _np
    import concourse.bacc as _bacc
    from concourse import mybir as _mybir
    from concourse.bass_utils import run_bass_kernel_spmd as _run

    nc = _bacc.Bacc("TRN2", target_bir_lowering=False, num_devices=1)
    arrays, args = {}, []
    for name in _INS:
        a = _np.ascontiguousarray(inputs[name])
        a = a.reshape(a.shape or (1,))
        arrays[f"in_{name}_dram"] = a
        args.append(nc.dram_tensor(f"in_{name}_dram", a.shape, _mybir.dt.from_np(a.dtype), kind="ExternalInput").ap())
    for i, (shape, dtype) in enumerate(_OUTS):
        dt = _mybir.dt.from_np(_np.dtype(dtype))
        args.append(nc.dram_tensor(f"out_{i}_dram", shape, dt, kind="ExternalOutput").ap())
    xattn_moe_kernel(nc, *args)
    r = _run(nc, [arrays], core_ids=[0])
    return _np.asarray(r.results[0]["out_0_dram"])
```

```python
from contextlib import ExitStack

import numpy as np

import concourse.bass as bass
from concourse import mybir

F32 = mybir.dt.float32
F16 = mybir.dt.float16
ALU = mybir.AluOpType
I32 = mybir.dt.int32
ACT = mybir.ActivationFunctionType
AX = mybir.AxisListType

P = 128
HEADS = 4
TOP_K_RATIO = 0.3
EPS = 1e-5
GROUPS, TOP_GROUPS, TOP_EXPERTS = 8, 4, 8
ROUTED_SCALE = 2.5
BISECTIONS = 26
LOWEST = -3.0e38
W_SCALE = 256.0


class Chain:

    def __init__(self, engine, sem, base=0):
        self.engine, self.sem, self.base, self.n = engine, sem, base, 0

    def done(self, instruction):
        self.n += 1
        instruction.then_inc(self.sem, 1)

    def settle(self):
        self.engine.wait_ge(self.sem, self.base + self.n)

    def step(self, instruction):
        self.done(instruction)
        self.settle()


def xattn_moe_kernel(nc, x, ctx_in, Wq, Wk, gamma_raw, router_w, router_bias, w_gate, w_up, w_down,
                     sw_gate, sw_up, sw_down, out):
    B, N, H = x.shape
    D = ctx_in.shape[2]
    E, _, I = w_gate.shape
    SI = sw_gate.shape[1]
    RT = N // P
    KC = H // P
    IC = I // P
    TT = B * RT
    SH = SI // I
    EG = E // GROUPS
    KEEP = max(1, int(N * TOP_K_RATIO))
    NT = TT * TOP_EXPERTS + E
    XG = 4
    QC = E * TT // P
    SIM_SCALE = 1.0 / (float(np.sqrt(np.float32(D // HEADS))) * HEADS)
    assert D == P and N == 512 and H == 512 and IC == 2

    with ExitStack() as stack:
        def sb(name, shape, dt=F32):
            return stack.enter_context(nc.sbuf_tensor(name, shape, dt))

        def sem(name):
            return stack.enter_context(nc.semaphore(name))

        bank = [stack.enter_context(nc.psum_tensor(f"bank{i}", [P, 512], F32)) for i in range(8)]

        xT16 = sb("xT16", [P, 2, KC, TT * P], F16)
        route = sb("route", [P, TT, E])
        acc = sb("acc", [P, TT, H])
        chosen = sb("chosen", [P, TT, E])
        ident = sb("ident", [P, P])
        xrows = nc.dram_tensor("xrows", [TT * P + P, H], F32).ap()
        table = nc.dram_tensor("table", [E * TT * P, 2], F32).ap()

        SEMS_B = ("cum_ready keys_ready records_ready scattered table_loaded counts_ready count_copied starts_ready "
                  "st_ready spread_ready onehot_ready ids_psum ids_copied tables_ready out_stored "
                  "b_wload b_whi b_wlo gathered0 gathered1 gathered2 gathered3 xgT_ready xg_hi xg_lo "
                  "b_gu b_silu b_hid b_hidT b_hhi b_hlo b_down y_ready added_rows pchain echain")

        names = ("consts ident_zero small_loaded ctx_loaded x_loaded wT_ready wT_copied ctxT_ready hT_ready "
                 "qk_ready qk_copied sim_ready sim_copied dve_chain act_chain pool_chain gamma_ready var_ready sqrt_ready "
                 "coef_ready base_ready sig_ready adj_ready adjT_ready adjT_used xn_ready xnT_ready xT32_ready "
                 "xhi_ready xlo_ready logits_ready scores_ready routed wload0 wload1 whi_ready wlo_ready gu_ready "
                 "silu_ready hid_ready hidT_ready hhi_ready hlo_ready down_ready added stored "
                 "rows_stored zeroed pool_consts "+SEMS_B).split()
        S = {n: sem(n) for n in names}

        phase = stack.enter_context(ExitStack())

        def sb(name, shape, dt=F32):
            return phase.enter_context(nc.sbuf_tensor(name, shape, dt))

        zeros = sb("zeros", [P, 2 * E * TT])
        w_qk = sb("w_qk", [P, 2, D])
        w_qkT = sb("w_qkT", [P, 2, D])
        gcol = sb("gcol", [P, 4])
        rw = sb("rw", [P, KC, E])
        bias = sb("bias", [P, E])
        ctx_sb = sb("ctx_sb", [P, RT, D])
        x_sb = sb("x_sb", [P, RT, H])
        base = sb("base", [P, RT, H])
        hT = sb("hT", [P, N])
        qT = sb("qT", [P, N])
        kT = sb("kT", [P, N])
        sim = sb("sim", [P, RT, N])
        adj = sb("adj", [P, RT, N])
        junk = sb("junk", [P, RT, N], mybir.dt.bfloat16)
        tmp = sb("tmp", [P, N])
        xn = sb("xn", [P, RT, H])
        xT32 = sb("xT32", [P, RT, KC, P])
        st6 = sb("st6", [P, RT, 6])
        mv = sb("mv", [P, RT, 2])
        ve = sb("ve", [P, RT])
        sd = sb("sd", [P, RT])
        rs = sb("rs", [P, RT])
        nt = sb("nt", [P, RT])
        nt2 = sb("nt2", [P, RT])
        coefA = sb("coefA", [P, RT])
        coefB = sb("coefB", [P, RT])
        mx = sb("mx", [P, RT])
        rng = sb("rng", [P, RT])
        lo = sb("lo", [P, RT])
        mid = sb("mid", [P, RT])
        cnt = sb("cnt", [P, RT])
        dlt = sb("dlt", [P, RT])
        scores = sb("scores", [P, RT, E])
        sg = sb("sg", [P, RT, E])
        pmx = sb("pmx", [P, RT, GROUPS, 2])
        pmn = sb("pmn", [P, RT, GROUPS, 2])
        t1 = sb("t1", [P, RT, GROUPS])
        t2 = sb("t2", [P, RT, GROUPS])
        t3 = sb("t3", [P, RT, GROUPS])
        gs = sb("gs", [P, RT, GROUPS + TOP_GROUPS])
        g8 = sb("g8", [P, RT, 8])
        gtaken = sb("gtaken", [P, RT, GROUPS + TOP_GROUPS])
        gkeep = sb("gkeep", [P, RT, GROUPS])
        masked = sb("masked", [P, RT, E])
        e8 = sb("e8", [P, RT, 8])
        etaken = sb("etaken", [P, RT, E])
        wsel = sb("wsel", [P, RT, E])
        wsum = sb("wsum", [P, RT])
        def _sl(b, i):
            return bass.ds(b * (RT * P) + i * P, P)

        def store_rows(sp, b):
            sp.wait_ge(S["xn_ready"], b + 1)
            sp.dma_start(xrows[b * N:(b + 1) * N, :].rearrange("(i p) h -> p i h", p=P), xn[:, :, :]).then_inc(S["rows_stored"], 16)

        with nc.Block() as block:
            @block.sync
            def _(sp):
                for i, w in enumerate((Wq, Wk)):
                    sp.dma_start(w_qk[:, i, :], w).then_inc(S["small_loaded"], 16)
                sp.dma_start(gcol[:, 0:1], gamma_raw.partition_broadcast(P)).then_inc(S["small_loaded"], 16)
                sp.dma_start(rw[:, :, :], router_w.rearrange("(k p) e -> p k e", p=P)).then_inc(S["small_loaded"], 16)
                sp.dma_start(bias[:, :], router_bias.partition_broadcast(P)).then_inc(S["small_loaded"], 16)
                sp.wait_ge(S["consts"], 3)
                sp.dma_start(xrows[TT * P:, :], zeros[:, 0:H]).then_inc(S["rows_stored"], 16)
                sp.dma_start(out[TT * P:, :], zeros[:, 0:H]).then_inc(S["zeroed"], 16)
                sp.dma_start(table.rearrange("(p s) a -> p (s a)", p=P), zeros[:, :]).then_inc(S["zeroed"], 16)
                for b in range(B):
                    sp.wait_ge(S["ctxT_ready"], b)
                    sp.dma_start(ctx_sb[:, :, :], ctx_in.rearrange("b (i p) d -> b p i d", p=P)[bass.ds(b, 1)].rearrange("b p i d -> (b p) i d")).then_inc(S["ctx_loaded"], 16)
                    sp.wait_ge(S["base_ready"], b * RT)
                    sp.dma_start(x_sb[:, :, :], x.rearrange("b (i p) h -> b p i h", p=P)[bass.ds(b, 1)].rearrange("b p i h -> (b p) i h")).then_inc(S["x_loaded"], 16)
                    if b >= 1:
                        store_rows(sp, b - 1)
                store_rows(sp, B - 1)
                sp.wait_ge(S["rows_stored"], 16 * (B + 1))
                sp.wait_ge(S["zeroed"], 32)

            @block.gpsimd
            def _(pool):
                nc.gpsimd.memset(ident[:, :], 0.0).then_inc(S["ident_zero"], 1)
                pool.wait_ge(S["ident_zero"], 1)
                nc.gpsimd.affine_select(out=ident[:, :], in_=ident[:, :], compare_op=ALU.not_equal, fill=1.0,
                                        base=0, pattern=[[-1, P]], channel_multiplier=1).then_inc(S["consts"], 1)
                nc.gpsimd.memset(zeros[:, :], 0.0).then_inc(S["consts"], 1)
                nc.gpsimd.memset(gs[:, :, GROUPS:], LOWEST).then_inc(S["consts"], 1)
                for b in range(B):
                    pool.wait_ge(S["coef_ready"], b + 1)
                    pool.wait_ge(S["x_loaded"], b * 16 + 16)
                    pool.wait_ge(S["xn_ready"], b)
                    for i in range(RT):
                        nc.gpsimd.tensor_scalar(base[:, i, :], x_sb[:, i, :], coefA[:, i:i + 1], coefB[:, i:i + 1],
                                                ALU.mult, ALU.add).then_inc(S["base_ready"], 1)

            @block.tensor
            def _(pe):
                pe.wait_ge(S["consts"], 1)
                pe.wait_ge(S["small_loaded"], 5 * 16)
                for i in range(2):
                    nc.tensor.transpose(bank[1][:, i * D:(i + 1) * D], w_qk[:, i, :], ident[:, :]).then_inc(S["wT_ready"], 1)
                pe.wait_ge(S["wT_copied"], 1)
                for b in range(B):
                    pe.wait_ge(S["ctx_loaded"], b * 16 + 16)
                    for i in range(RT):
                        t = nc.tensor.transpose(bank[0][:, i * P:(i + 1) * P], ctx_sb[:, i, :], ident[:, :])
                    t.then_inc(S["ctxT_ready"], 1)
                    pe.wait_ge(S["hT_ready"], b + 1)
                    for i in range(2):
                        nc.tensor.matmul(bank[1 + i][:, :], w_qkT[:, i, :], hT[:, :], start=True, stop=True).then_inc(S["qk_ready"], 1)
                    pe.wait_ge(S["qk_copied"], 2 * b + 2)
                    for i in range(RT):
                        nc.tensor.matmul(bank[3 + i][:, :], qT[:, i * P:(i + 1) * P], kT[:, :], start=True, stop=True).then_inc(S["sim_ready"], 1)
                    pe.wait_ge(S["adj_ready"], RT * b + RT)
                    pe.wait_ge(S["sim_copied"], RT * b + RT)
                    for i in range(RT):
                        for j in range(RT):
                            t = nc.tensor.transpose(bank[3 + i][:, j * P:(j + 1) * P], adj[:, j, i * P:(i + 1) * P], ident[:, :])
                        t.then_inc(S["adjT_ready"], 1)
                    pe.wait_ge(S["xn_ready"], b + 1)
                    for i in range(RT):
                        if i >= 2:
                            pe.wait_ge(S["xlo_ready"], RT * b + i - 1)
                        for k in range(KC):
                            t = nc.tensor.transpose(bank[1 + i % 2][:, k * P:(k + 1) * P], xn[:, i, k * P:(k + 1) * P], ident[:, :])
                        t.then_inc(S["xnT_ready"], 1)
                    for i in range(RT):
                        pe.wait_ge(S["xT32_ready"], RT * b + i + 1)
                        for k in range(KC):
                            t = nc.tensor.matmul(bank[7][:, i * E:(i + 1) * E], xT32[:, i, k, :], rw[:, k, :],
                                                 start=(k == 0), stop=(k == KC - 1))
                    t.then_inc(S["logits_ready"], 1)
                    pe.wait_ge(S["scores_ready"], b + 1)

            @block.scalar
            def _(act):
                act.wait_ge(S["small_loaded"], 5 * 16)
                nc.scalar.activation(gcol[:, 1:2], gcol[:, 0:1], ACT.Sigmoid).then_inc(S["gamma_ready"], 1)
                for b in range(B):
                    act.wait_ge(S["var_ready"], 2 * b + 1)
                    nc.scalar.activation(sd[:, :], ve[:, :], ACT.Sqrt).then_inc(S["sqrt_ready"], 1)
                    act.wait_ge(S["qk_ready"], 2 * b + 2)
                    nc.scalar.copy(kT[:, :], bank[2][:, :]).then_inc(S["qk_copied"], 1)
                    act.wait_ge(S["adj_ready"], RT * b)
                    act.wait_ge(S["adjT_ready"], RT * b)
                    act.wait_ge(S["adjT_used"], RT * b)
                    for i in range(RT):
                        act.wait_ge(S["sim_ready"], RT * b + i + 1)
                        nc.scalar.mul(sim[:, i, :], bank[3 + i][:, :], SIM_SCALE).then_inc(S["sim_copied"], 1)
                    act.wait_ge(S["sim_copied"], RT * b + RT)
                    nc.scalar.activation(adj[:, :, :], sim[:, :, :], ACT.Sigmoid).then_inc(S["sig_ready"], 1)
                    act.wait_ge(S["var_ready"], 2 * b + 2)
                    nc.scalar.activation(sd[:, :], ve[:, :], ACT.Sqrt).then_inc(S["sqrt_ready"], 1)
                    for i in range(RT):
                        act.wait_ge(S["xnT_ready"], RT * b + i + 1)
                        act.wait_ge(S["xT32_ready"], RT * b + i + 1)
                        nc.scalar.copy(xT16[:, 0, :, _sl(b, i)],
                                       xT32[:, i, :, :]).then_inc(S["xhi_ready"], 1)
                    act.wait_ge(S["logits_ready"], b + 1)
                    nc.scalar.activation(scores[:, :, :], bank[7][:, 0:RT * E].rearrange("p (i e) -> p i e", e=E),
                                         ACT.Sigmoid).then_inc(S["scores_ready"], 1)

            @block.vector
            def _(dve):
                for i in range(2):
                    pass
                dve.wait_ge(S["wT_ready"], 2)
                nc.vector.tensor_copy(w_qkT[:, :, :], bank[1][:, 0:2 * D].rearrange("p (a d) -> p a d", a=2)).then_inc(S["wT_copied"], 1)
                dve.wait_ge(S["gamma_ready"], 1)
                pre = Chain(dve, S["dve_chain"])
                pre.done(nc.vector.tensor_scalar(gcol[:, 2:3], gcol[:, 1:2], -1.0, 1.0, ALU.mult, ALU.add))
                pre.step(nc.vector.tensor_scalar(gcol[:, 3:4], gcol[:, 1:2], 0.5, None, ALU.mult))
                dve.wait_ge(S["consts"], 3)

                def batch(b, per_batch):
                    v = nc.vector
                    ch = Chain(dve, S["dve_chain"], b * per_batch + pre.n)

                    def inverse_std(nth):
                        for i in range(RT):
                            ch.done(v.bn_aggr(mv[:, i, :], st6[:, i, :]))
                        ch.settle()
                        v.tensor_scalar(ve[:, :], mv[:, :, 1], EPS, None, ALU.add).then_inc(S["var_ready"], 1)
                        dve.wait_ge(S["sqrt_ready"], 2 * b + nth)
                        ch.step(v.reciprocal(rs[:, :], sd[:, :]))
                        ch.step(v.tensor_tensor(nt[:, :], rs[:, :], rs[:, :], ALU.mult))
                        ch.step(v.tensor_tensor(nt2[:, :], nt[:, :], ve[:, :], ALU.mult))
                        ch.step(v.tensor_scalar(nt[:, :], nt2[:, :], -0.5, 1.5, ALU.mult, ALU.add))
                        ch.step(v.tensor_tensor(rs[:, :], rs[:, :], nt[:, :], ALU.mult))

                    dve.wait_ge(S["ctxT_ready"], b + 1)
                    v.tensor_copy(hT[:, :], bank[0][:, :]).then_inc(S["hT_ready"], 1)
                    dve.wait_ge(S["x_loaded"], b * 16 + 16)
                    for i in range(RT):
                        ch.done(v.bn_stats(st6[:, i, :], x_sb[:, i, :]))
                    ch.settle()
                    dve.wait_ge(S["qk_ready"], 2 * b + 2)
                    v.tensor_copy(qT[:, :], bank[1][:, :]).then_inc(S["qk_copied"], 1)
                    inverse_std(1)
                    ch.step(v.tensor_scalar(nt[:, :], rs[:, :], gcol[:, 2:3], None, ALU.mult))
                    ch.done(v.tensor_scalar(coefA[:, :], nt[:, :], 1.0, None, ALU.add))
                    v.scalar_tensor_tensor(coefB[:, :], nt[:, :], -1.0, mv[:, :, 0], ALU.mult, ALU.mult).then_inc(S["coef_ready"], 1)

                    dve.wait_ge(S["sim_copied"], RT * b + RT)
                    ch.done(v.tensor_reduce(mx[:, :], sim[:, :, :], AX.X, ALU.max))
                    ch.step(v.tensor_reduce(lo[:, :], sim[:, :, :], AX.X, ALU.min))
                    ch.step(v.tensor_tensor(rng[:, :], mx[:, :], lo[:, :], ALU.subtract))
                    ch.step(v.tensor_scalar(rng[:, :], rng[:, :], 0.5, None, ALU.mult))
                    per = RT + 4
                    before = ch.n
                    with dve.Fori(0, BISECTIONS) as it:
                        inner = Chain(dve, S["dve_chain"], b * per_batch + it * per + (pre.n + before))
                        inner.step(v.tensor_tensor(mid[:, :], lo[:, :], rng[:, :], ALU.add))
                        for i in range(RT):
                            inner.done(v.tensor_scalar(junk[:, i, :], sim[:, i, :], mid[:, i:i + 1], 0.0, ALU.is_ge, ALU.add,
                                                       accum_out=cnt[:, i:i + 1]))
                        inner.settle()
                        inner.step(v.scalar_tensor_tensor(dlt[:, :], cnt[:, :], KEEP - 0.5, rng[:, :], ALU.is_ge, ALU.mult))
                        inner.done(v.tensor_tensor(lo[:, :], lo[:, :], dlt[:, :], ALU.add))
                        inner.step(v.tensor_scalar(rng[:, :], rng[:, :], 0.5, None, ALU.mult))
                        assert inner.n == per
                    ch.n = before + per * BISECTIONS

                    dve.wait_ge(S["sig_ready"], b + 1)
                    for i in range(RT):
                        v.scalar_tensor_tensor(adj[:, i, :], sim[:, i, :], lo[:, i:i + 1], adj[:, i, :],
                                               ALU.is_ge, ALU.mult).then_inc(S["adj_ready"], 1)
                    dve.wait_ge(S["adj_ready"], RT * b + RT)
                    dve.wait_ge(S["base_ready"], RT * b + RT)
                    for i in range(RT):
                        dve.wait_ge(S["adjT_ready"], RT * b + i + 1)
                        v.tensor_tensor(tmp[:, :], adj[:, i, :], bank[3 + i][:, :], ALU.add).then_inc(S["adjT_used"], 1)
                        dve.wait_ge(S["adjT_used"], RT * b + i + 1)
                        ch.step(v.scalar_tensor_tensor(acc[:, bass.ds(b * RT + i, 1), :].rearrange("p a h -> p (a h)"), tmp[:, :], gcol[:, 3:4], base[:, i, :],
                                                       ALU.mult, ALU.add))
                        ch.done(v.bn_stats(st6[:, i, :], acc[:, bass.ds(b * RT + i, 1), :].rearrange("p a h -> p (a h)")))
                    ch.settle()
                    inverse_std(2)
                    dve.wait_ge(S["rows_stored"], 16 * b + 16)
                    for i in range(RT):
                        t = v.tensor_scalar(xn[:, i, :], acc[:, bass.ds(b * RT + i, 1), :].rearrange("p a h -> p (a h)"), mv[:, i, 0:1], rs[:, i:i + 1],
                                            ALU.subtract, ALU.mult)
                        if i < RT - 1:
                            ch.done(t)
                    t.then_inc(S["xn_ready"], 1)
                    for i in range(RT):
                        dve.wait_ge(S["xnT_ready"], RT * b + i + 1)
                        v.tensor_copy(xT32[:, i, :, :], bank[1 + i % 2][:, :].rearrange("p (k t) -> p k t", k=KC)).then_inc(S["xT32_ready"], 1)
                        dve.wait_ge(S["xhi_ready"], RT * b + i + 1)
                        v.tensor_tensor(xT16[:, 1, :, _sl(b, i)], xT32[:, i, :, :], xT16[:, 0, :, _sl(b, i)],
                                        ALU.subtract).then_inc(S["xlo_ready"], 1)

                    dve.wait_ge(S["scores_ready"], b + 1)
                    ch.step(v.tensor_tensor(sg[:, :, :], scores[:, :, :], bias[:, :].unsqueeze(1).to_broadcast([P, RT, E]), ALU.add))
                    q = sg[:, :, :].rearrange("p i (g a c) -> p i g a c", a=2, c=2)
                    for c in range(RT):
                        ch.done(v.tensor_tensor(pmx[:, c, :, :], q[:, c, :, :, 0], q[:, c, :, :, 1], ALU.max))
                        ch.done(v.tensor_tensor(pmn[:, c, :, :], q[:, c, :, :, 0], q[:, c, :, :, 1], ALU.min))
                    ch.settle()
                    ch.done(v.tensor_tensor(t1[:, :, :], pmx[:, :, :, 0], pmx[:, :, :, 1], ALU.max))
                    ch.done(v.tensor_tensor(t2[:, :, :], pmx[:, :, :, 0], pmx[:, :, :, 1], ALU.min))
                    ch.step(v.tensor_tensor(t3[:, :, :], pmn[:, :, :, 0], pmn[:, :, :, 1], ALU.max))
                    ch.step(v.tensor_tensor(t2[:, :, :], t2[:, :, :], t3[:, :, :], ALU.max))
                    ch.step(v.tensor_tensor(gs[:, :, 0:GROUPS], t1[:, :, :], t2[:, :, :], ALU.add))
                    for i in range(RT):
                        ch.done(v.max(g8[:, i, :], gs[:, i, 0:GROUPS]))
                    ch.settle()
                    ch.step(v.memset(g8[:, :, TOP_GROUPS:], LOWEST))
                    for i in range(RT):
                        ch.done(v.match_replace(gtaken[:, i, :], g8[:, i, :], gs[:, i, :], LOWEST))
                    ch.settle()
                    ch.step(v.tensor_scalar(gkeep[:, :, :], gtaken[:, :, 0:GROUPS], LOWEST / 2, None, ALU.is_le))
                    for i in range(RT):
                        ch.done(v.tensor_tensor(masked[:, i, :].rearrange("p (g c) -> p g c", c=EG), sg[:, i, :].rearrange("p (g c) -> p g c", c=EG),
                                                gkeep[:, i, :].unsqueeze(2).to_broadcast([P, GROUPS, EG]), ALU.mult))
                    ch.settle()
                    for i in range(RT):
                        ch.done(v.max(e8[:, i, :], masked[:, i, :]))
                    ch.settle()
                    for i in range(RT):
                        ch.done(v.match_replace(etaken[:, i, :], e8[:, i, :], masked[:, i, :], LOWEST))
                    ch.settle()
                    ch.done(v.tensor_scalar(chosen[:, b * RT:(b + 1) * RT, :], etaken[:, :, :], LOWEST / 2, None, ALU.is_le))
                    ch.step(v.scalar_tensor_tensor(wsel[:, :, :], etaken[:, :, :], LOWEST / 2, scores[:, :, :], ALU.is_le, ALU.mult))
                    ch.step(v.tensor_reduce(wsum[:, :], wsel[:, :, :], AX.X, ALU.add))
                    ch.step(v.reciprocal(wsum[:, :], wsum[:, :]))
                    for i in range(RT):
                        t = v.tensor_scalar(route[:, bass.ds(b * RT + i, 1), 0:E].rearrange("p a e -> p (a e)"), wsel[:, i, :], wsum[:, i:i + 1], ROUTED_SCALE, ALU.mult, ALU.mult)
                        if i < RT - 1:
                            ch.done(t)
                    t.then_inc(S["routed"], 1)
                    return ch.n

                PER_BATCH = 290
                for b in range(B):
                    n = batch(b, PER_BATCH)
                    assert n == PER_BATCH, n

        phase.close()

        stage_gu = sb("stage_gu", [P, KC, 2, I])
        stage_dn = sb("stage_dn", [P, IC, H])
        gu16 = sb("gu16", [P, 2, 2, KC, 2 * I], F16)
        dn16 = sb("dn16", [P, 2, 2, IC, H], F16)
        silu = sb("silu", [P, 2, I])
        hid = sb("hid", [P, 2, I])
        hT16 = sb("hT16", [P, 2, 2, I], F16)
        xg = sb("xg", [P, XG, H])
        xgT = sb("xgT", [P, 2, 2, KC, P], F16)
        y = sb("y", [P, 2, H])
        before = sb("before", [P, P])
        ones = sb("ones", [P, P])
        slot_base = sb("slot_base", [P, E], I32)
        slot_basef = sb("slot_basef", [P, E])
        row_id = sb("row_id", [P, TT], I32)
        row_idf = sb("row_idf", [P, TT])
        trash = sb("trash", [P, 1], I32)
        trashf = sb("trashf", [P, 1])
        tile_no = sb("tile_no", [P, NT], I32)
        tile_nof = sb("tile_nof", [P, NT])
        j_of = sb("j_of", [P, 1], I32)
        j_off = sb("j_off", [P, 1])
        expand = sb("expand", [E, TT * E])
        carry = sb("carry", [P, 2, TT, E])
        key = sb("key", [P, TT, E])
        key8 = sb("key8", [P, TT, TOP_EXPERTS])
        key8i = sb("key8i", [P, TT, TOP_EXPERTS], I32)
        match = sb("match", [P, 2, TOP_EXPERTS, E])
        matchw = sb("matchw", [P, 2, TOP_EXPERTS, E])
        record = sb("record", [P, TT, TOP_EXPERTS, 2])
        tab = sb("tab", [P, QC, P, 2])
        n_e = sb("n_e", [E, 1])
        n_i = sb("n_i", [E, 1], I32)
        n_t = sb("n_t", [E, 1], I32)
        st = sb("st", [E, 2])
        spread = sb("spread", [P, QC, 2])
        live = sb("live", [P, QC])
        target = sb("target", [P, QC])
        onehot = sb("onehot", [P, QC, NT])
        steps = sb("steps", [E, 2, NT])
        pad = sb("pad", [P, NT])
        ids = sb("ids", [P, NT])
        ids_i = sb("ids_i", [P, NT], I32)
        wts = sb("wts", [P, NT])
        tile_info = sb("tile_info", [1, 2, NT], I32)

        GU, HT, DN = (0, 1), (2, 3), (4, 5)
        XB = (6, 7)
        SN = SH * TT

        def three(out_ap, stationary, moving, chunks):
            parts = [(0, 0), (0, 1), (1, 0)]
            for c in range(chunks):
                for a, w in parts:
                    last = nc.tensor.matmul(out_ap, stationary(a, c), moving(w, c), start=(c == 0 and (a, w) == parts[0]),
                                            stop=(c == chunks - 1 and (a, w) == parts[-1]))
            return last

        with nc.Block() as block:
            @block.sync
            def _(sp):
                def load(n, g, u, d):
                    if not (isinstance(n, int) and n == 0):
                        sp.wait_ge(S["b_wlo"], 2 * n)
                    sp.dma_start(stage_gu[:, :, 0, :], g.rearrange("(k p) i -> p k i", p=P)).then_inc(S["b_wload"], 16)
                    sp.dma_start(stage_gu[:, :, 1, :], u.rearrange("(k p) i -> p k i", p=P)).then_inc(S["b_wload"], 16)
                    sp.dma_start(stage_dn[:, :, :], d.rearrange("(k p) h -> p k h", p=P)).then_inc(S["b_wload"], 16)

                for h in range(SH):
                    c = slice(h * I, (h + 1) * I)
                    load(h, sw_gate[:, c], sw_up[:, c], sw_down[c, :])
                load(SH, w_gate[0], w_up[0], w_down[0])
                sp.wait_ge(S["scattered"], 16 * TT * TOP_EXPERTS)
                sp.dma_start(tab[:, :, :, :].rearrange("p c s a -> p c (s a)"), table.rearrange("(c p s) a -> p c (s a)", p=P, s=P)).then_inc(S["table_loaded"], 16)
                sp.wait_ge(S["added"], SN)
                sp.dma_start(out[0:TT * P, :].rearrange("(g p) h -> p g h", p=P), acc[:, :, :]).then_inc(S["out_stored"], 16)
                with sp.Fori(1, E) as e:
                    load(e + SH, *(w[bass.ds(e, 1)].rearrange("a k n -> (a k) n") for w in (w_gate, w_up, w_down)))

            @block.gpsimd
            def _(pool):
                g_ = nc.gpsimd
                ch = Chain(pool, S["echain"])
                ch.done(g_.memset(ones[:, :], 1.0))
                ch.done(g_.memset(before[:, :], 1.0))
                ch.done(g_.memset(expand[:, :], 1.0))
                ch.done(g_.iota(slot_base[:, :], [[TT * P, E]], base=1, channel_multiplier=0))
                ch.done(g_.iota(row_id[:, :], [[P, TT]], base=1, channel_multiplier=1))
                ch.done(g_.iota(trash[:, :], [[0, 1]], base=TT * P + 1, channel_multiplier=1))
                ch.done(g_.iota(tile_no[:, :], [[1, NT]], base=0, channel_multiplier=0))
                ch.done(g_.iota(j_of[:, :], [[0, 1]], base=0, channel_multiplier=1))
                ch.settle()
                ch.done(g_.affine_select(out=before[:, :], in_=before[:, :], compare_op=ALU.is_ge, fill=0.0, base=-1,
                                         pattern=[[1, P]], channel_multiplier=-1))
                ch.step(g_.affine_select(out=expand[:, :], in_=expand[:, :], compare_op=ALU.is_ge, fill=0.0, base=0,
                                         pattern=[[1, TT * E]], channel_multiplier=-TT))
                g_.affine_select(out=expand[:, :], in_=expand[:, :], compare_op=ALU.is_ge, fill=0.0, base=TT - 1,
                                 pattern=[[-1, TT * E]], channel_multiplier=TT).then_inc(S["pool_consts"], 1)
                for g in range(TT):
                    pool.wait_ge(S["records_ready"], g + 1)
                    if g == 0:
                        pool.wait_ge(S["zeroed"], 32)
                    for k in range(TOP_EXPERTS):
                        g_.indirect_dma_start(table, bass.IndirectOffsetOnAxis(ap=key8i[:, g, k:k + 1], axis=0),
                                              record[:, g, k, :], None).then_inc(S["scattered"], 16)
                pool.wait_ge(S["tables_ready"], 1)
                pool.wait_ge(S["rows_stored"], 16 * (B + 1))
                pool.wait_ge(S["zeroed"], 32)

                def gather(t):
                    if t >= XG:
                        pool.wait_ge(S["xgT_ready"], t - XG + 1)
                    g_.indirect_dma_start(xg[:, t % XG, :], None, xrows,
                                          bass.IndirectOffsetOnAxis(ap=ids_i[:, t:t + 1], axis=0)).then_inc(S[f"gathered{t % XG}"], 16)

                def scatter(t):
                    pool.wait_ge(S["y_ready"], t + 1)
                    if t >= 1:
                        pool.wait_ge(S["added_rows"], t * 16)
                    g_.indirect_dma_start(out, bass.IndirectOffsetOnAxis(ap=ids_i[:, t:t + 1], axis=0), y[:, t % 2, :], None,
                                          compute_op=ALU.add).then_inc(S["added_rows"], 16)

                for t in range(XG):
                    gather(t)
                pool.wait_ge(S["out_stored"], 16)
                for t in range(NT):
                    if t + XG < NT:
                        gather(t + XG)
                    scatter(t)
                pool.wait_ge(S["added_rows"], NT * 16)

            @block.scalar
            def _(act):
                a_ = nc.scalar

                def convert(n, slot):
                    act.wait_ge(S["b_wload"], n * 48 + 48)
                    if isinstance(slot, int):
                        go, do = gu16[:, slot, 0, :, :], dn16[:, slot, 0, :, :]
                    else:
                        go = gu16[:, bass.ds(slot, 1), 0, :, :].rearrange("p a k n -> p (a k) n")
                        do = dn16[:, bass.ds(slot, 1), 0, :, :].rearrange("p a k n -> p (a k) n")
                    a_.mul(go, stage_gu[:, :, :, :].rearrange("p k a i -> p k (a i)"), W_SCALE).then_inc(S["b_whi"], 1)
                    a_.mul(do, stage_dn[:, :, :], W_SCALE).then_inc(S["b_whi"], 1)

                def shared(n, s, first=False):
                    act.wait_ge(S["gu_ready"], n + 1)
                    if not first:
                        act.wait_ge(S["hid_ready"], n - 1)
                    a_.activation(silu[:, s, :], bank[GU[s]][:, 0:I], ACT.Silu, scale=1.0 / W_SCALE).then_inc(S["silu_ready"], 1)
                    act.wait_ge(S["hidT_ready"], n + 1)
                    if not first:
                        act.wait_ge(S["down_ready"], n - 1)
                    a_.copy(hT16[:, s, 0, :], bank[HT[s]][:, 0:I]).then_inc(S["hhi_ready"], 1)

                for h in range(SH):
                    convert(h, h % 2)
                    for n in range(2):
                        shared(h * TT + n, n, first=(h == 0))
                    with act.Fori(2, TT - 1, 2) as g:
                        for s in range(2):
                            shared(g + (s + h * TT), s)
                act.wait_ge(S["down_ready"], SN - TT)
                convert(SH, SH % 2)
                act.wait_ge(S["tables_ready"], 1)

                def split_rows(t, s):
                    act.wait_ge(S["xgT_ready"], t + 1)
                    if not (isinstance(t, int) and t < 2):
                        act.wait_ge(S["b_gu"], t - 1)
                    a_.copy(xgT[:, s, 0, :, :], bank[XB[s]][:, :].rearrange("p (k t) -> p k t", k=KC)).then_inc(S["xg_hi"], 1)

                def routed(t, s, first=False):
                    act.wait_ge(S["b_gu"], t + 1)
                    if not first:
                        act.wait_ge(S["b_hid"], t - 1)
                    a_.activation(silu[:, s, :], bank[GU[s]][:, 0:I], ACT.Silu, scale=1.0 / W_SCALE).then_inc(S["b_silu"], 1)
                    act.wait_ge(S["b_hidT"], t + 1)
                    if not first:
                        act.wait_ge(S["b_down"], t - 1)
                    a_.copy(hT16[:, s, 0, :], bank[HT[s]][:, 0:I]).then_inc(S["b_hhi"], 1)

                def result(t, s, first=False):
                    act.wait_ge(S["b_down"], t + 1)
                    if not first:
                        act.wait_ge(S["added_rows"], (t - 1) * 16)
                    w = wts[:, t:t + 1] if isinstance(t, int) else wts[:, bass.ds(t, 1)]
                    a_.activation(y[:, s, :], bank[DN[s]][:, :], ACT.Identity, scale=w).then_inc(S["y_ready"], 1)

                def next_weights(t):
                    f = act.value_load(tile_info[0:1, 1, bass.ds(t, 1)] if not isinstance(t, int) else tile_info[0:1, 1, t:t + 1], min_val=0, max_val=1)
                    with act.If(f > 0):
                        e = act.value_load(tile_info[0:1, 0, bass.ds(t, 1)] if not isinstance(t, int) else tile_info[0:1, 0, t:t + 1], min_val=0, max_val=E - 1)
                        convert(e + (SH + 1), (e + (SH + 1)) % 2)

                split_rows(0, 0)
                split_rows(1, 1)
                routed(0, 0, first=True)
                next_weights(0)
                split_rows(2, 0)
                routed(1, 1, first=True)
                next_weights(1)
                result(0, 0, first=True)
                with act.Fori(2, NT - 3, 2) as t:
                    for s in range(2):
                        split_rows(t + (s + 1), 1 - s)
                        routed(t + s, s)
                        next_weights(t + s)
                        result(t + (s - 1), 1 - s)
                split_rows(NT - 1, 1)
                routed(NT - 2, 0)
                result(NT - 3, 1)
                routed(NT - 1, 1)
                result(NT - 2, 0)
                result(NT - 1, 1)

            @block.vector
            def _(dve):
                v = nc.vector
                ch = Chain(dve, S["pchain"])
                dve.wait_ge(S["pool_consts"], 1)
                ch.done(v.tensor_copy(slot_basef[:, :], slot_base[:, :]))
                ch.done(v.tensor_copy(row_idf[:, :], row_id[:, :]))
                ch.done(v.tensor_copy(trashf[:, :], trash[:, :]))
                ch.done(v.tensor_copy(tile_nof[:, :], tile_no[:, :]))
                ch.step(v.tensor_scalar(j_of[:, :], j_of[:, :], TT - 1, None, ALU.bitwise_and))
                ch.step(v.tensor_copy(j_off[:, :], j_of[:, :]))
                dve.wait_ge(S["cum_ready"], 2)
                ch.done(v.memset(carry[:, 0, 0:1, :], 0.0))
                ch.step(v.tensor_copy(carry[:, 0, 1:TT, :], bank[1][:, 0:(TT - 1) * E].rearrange("p (g e) -> p g e", e=E)))
                cur, d = 0, 1
                while d < TT:
                    ch.done(v.tensor_copy(carry[:, 1 - cur, 0:d, :], carry[:, cur, 0:d, :]))
                    ch.step(v.tensor_tensor(carry[:, 1 - cur, d:, :], carry[:, cur, d:, :], carry[:, cur, 0:TT - d, :], ALU.add))
                    cur, d = 1 - cur, 2 * d
                ch.step(v.tensor_tensor(key[:, :, :], carry[:, cur, :, :], bank[0][:, :].rearrange("p (g e) -> p g e", e=E), ALU.add))
                ch.step(v.tensor_tensor(key[:, :, :], key[:, :, :], slot_basef[:, :].unsqueeze(1).to_broadcast([P, TT, E]), ALU.add))
                ch.step(v.tensor_tensor(key[:, :, :], key[:, :, :], chosen[:, :, :], ALU.mult))
                for g in range(TT):
                    ch.done(v.max(key8[:, g, :], key[:, g, :]))
                ch.settle()
                ch.done(v.tensor_scalar(key8i[:, :, :], key8[:, :, :], -1.0, None, ALU.add))
                for g in range(TT):
                    m, mw = match[:, g % 2], matchw[:, g % 2]
                    ch.step(v.tensor_tensor(m, key8[:, g, :].unsqueeze(2).to_broadcast([P, TOP_EXPERTS, E]),
                                            key[:, g, :].unsqueeze(1).to_broadcast([P, TOP_EXPERTS, E]), ALU.is_equal))
                    ch.step(v.tensor_tensor(mw, m, route[:, g, :].unsqueeze(1).to_broadcast([P, TOP_EXPERTS, E]), ALU.mult))
                    ch.done(v.tensor_copy(record[:, g, :, 0], row_idf[:, g:g + 1].to_broadcast([P, TOP_EXPERTS])))
                    ch.step(v.tensor_reduce(record[:, g, :, 1], mw, AX.X, ALU.add))
                    v.tensor_scalar(record[:, g, :, 1], record[:, g, :, 1], 1.0 / W_SCALE, None, ALU.mult).then_inc(S["records_ready"], 1)
                dve.wait_ge(S["counts_ready"], 1)
                ch.step(v.tensor_scalar(n_e[:, :], bank[2][0:E, 0:1], P - 1.0, None, ALU.add))
                ch.step(v.tensor_copy(n_i[:, :], n_e[:, :]))
                ch.step(v.tensor_scalar(n_t[:, :], n_i[:, :], 7, None, ALU.arith_shift_right))
                ch.step(v.tensor_copy(n_e[:, :], n_t[:, :]))
                v.tensor_scalar(st[:, 1:2], n_e[:, :], 1.0, None, ALU.max).then_inc(S["count_copied"], 1)
                dve.wait_ge(S["starts_ready"], 1)
                v.tensor_copy(st[:, 0:1], bank[3][0:E, 0:1]).then_inc(S["st_ready"], 1)
                dve.wait_ge(S["st_ready"], 1)
                ch.done(v.tensor_scalar(steps[:, 0, :], tile_nof[0:E, :], st[:, 0:1], None, ALU.is_ge))
                ch.done(v.tensor_scalar(steps[:, 1, :], tile_nof[0:E, :], st[:, 0:1], None, ALU.is_equal))
                dve.wait_ge(S["spread_ready"], 1)
                ch.step(v.tensor_copy(spread[:, :, :], bank[4][:, 0:2 * QC].rearrange("p (c a) -> p c a", a=2)))
                ch.done(v.tensor_scalar(live[:, :], spread[:, :, 1], j_off[:, 0:1], None, ALU.is_gt))
                ch.step(v.tensor_scalar(target[:, :], spread[:, :, 0], j_off[:, 0:1], 1.0, ALU.add, ALU.add))
                ch.step(v.tensor_tensor(target[:, :], target[:, :], live[:, :], ALU.mult))
                ch.step(v.tensor_scalar(target[:, :], target[:, :], -1.0, None, ALU.add))
                for c in range(QC):
                    t = v.tensor_scalar(onehot[:, c, :], tile_nof[:, :], target[:, c:c + 1], None, ALU.is_equal)
                    if c < QC - 1:
                        ch.done(t)
                t.then_inc(S["onehot_ready"], 1)

                def convert(n, slot):
                    dve.wait_ge(S["b_whi"], 2 * n + 2)
                    if isinstance(slot, int):
                        parts = [(w[:, slot, 0].rearrange("p k n -> p (k n)"), w[:, slot, 1].rearrange("p k n -> p (k n)")) for w in (gu16, dn16)]
                    else:
                        parts = [(w[:, bass.ds(slot, 1), 0].rearrange("p a k n -> p (a k n)"), w[:, bass.ds(slot, 1), 1].rearrange("p a k n -> p (a k n)")) for w in (gu16, dn16)]
                    for (hi, low), src in zip(parts, (stage_gu[:, :, :, :].rearrange("p k a i -> p (k a i)"), stage_dn[:, :, :].rearrange("p k n -> p (k n)"))):
                        v.scalar_tensor_tensor(low, src, W_SCALE, hi, ALU.mult, ALU.subtract).then_inc(S["b_wlo"], 1)

                def shared(n, g, s, first=False):
                    dve.wait_ge(S["silu_ready"], n + 1)
                    if not first:
                        dve.wait_ge(S["hidT_ready"], n - 1)
                    v.scalar_tensor_tensor(hid[:, s, :], bank[GU[s]][:, I:2 * I], 1.0 / W_SCALE, silu[:, s, :],
                                           ALU.mult, ALU.mult).then_inc(S["hid_ready"], 1)
                    dve.wait_ge(S["hhi_ready"], n + 1)
                    v.tensor_tensor(hT16[:, s, 1, :], bank[HT[s]][:, 0:I], hT16[:, s, 0, :], ALU.subtract).then_inc(S["hlo_ready"], 1)
                    dve.wait_ge(S["down_ready"], n + 1)
                    a = acc[:, g, :] if isinstance(g, int) else acc[:, bass.ds(g, 1), :].rearrange("p a h -> p (a h)")
                    v.scalar_tensor_tensor(a, bank[DN[s]][:, :], 1.0 / W_SCALE, a, ALU.mult, ALU.add).then_inc(S["added"], 1)

                for h in range(SH):
                    convert(h, h % 2)
                    for n in range(2):
                        shared(h * TT + n, n, n, first=(h == 0))
                    with dve.Fori(2, TT - 1, 2) as g:
                        for s in range(2):
                            shared(g + (s + h * TT), g + s, s)
                convert(SH, SH % 2)
                dve.wait_ge(S["ids_psum"], 1)
                ch.step(v.tensor_copy(ids[:, :], bank[6][:, 0:NT]))
                ch.done(v.tensor_copy(wts[:, :], bank[6][:, NT:2 * NT]))
                ch.step(v.tensor_scalar(pad[:, :], ids[:, :], 0.0, trashf[:, 0:1], ALU.is_le, ALU.mult))
                ch.step(v.scalar_tensor_tensor(ids[:, :], ids[:, :], -1.0, pad[:, :], ALU.add, ALU.add))
                ch.done(v.tensor_copy(ids_i[:, :], ids[:, :]))
                ch.done(v.tensor_scalar(tile_info[0:1, 0, :], bank[7][0:1, 0:NT], -1.0, None, ALU.add))
                ch.settle()
                v.tensor_copy(tile_info[0:1, 1, :], bank[7][0:1, NT:2 * NT]).then_inc(S["tables_ready"], 1)

                def split_rows(t, s):
                    dve.wait_ge(S["xg_hi"], t + 1)
                    v.tensor_tensor(xgT[:, s, 1, :, :], bank[XB[s]][:, :].rearrange("p (k t) -> p k t", k=KC), xgT[:, s, 0, :, :],
                                    ALU.subtract).then_inc(S["xg_lo"], 1)

                def routed(t, s, first=False):
                    dve.wait_ge(S["b_silu"], t + 1)
                    if not first:
                        dve.wait_ge(S["b_hidT"], t - 1)
                    v.scalar_tensor_tensor(hid[:, s, :], bank[GU[s]][:, I:2 * I], 1.0 / W_SCALE, silu[:, s, :],
                                           ALU.mult, ALU.mult).then_inc(S["b_hid"], 1)
                    dve.wait_ge(S["b_hhi"], t + 1)
                    v.tensor_tensor(hT16[:, s, 1, :], bank[HT[s]][:, 0:I], hT16[:, s, 0, :], ALU.subtract).then_inc(S["b_hlo"], 1)

                def next_weights(t):
                    f = dve.value_load(tile_info[0:1, 1, bass.ds(t, 1)] if not isinstance(t, int) else tile_info[0:1, 1, t:t + 1], min_val=0, max_val=1)
                    with dve.If(f > 0):
                        e = dve.value_load(tile_info[0:1, 0, bass.ds(t, 1)] if not isinstance(t, int) else tile_info[0:1, 0, t:t + 1], min_val=0, max_val=E - 1)
                        convert(e + (SH + 1), (e + (SH + 1)) % 2)

                dve.wait_ge(S["tables_ready"], 1)
                split_rows(0, 0)
                split_rows(1, 1)
                routed(0, 0, first=True)
                next_weights(0)
                split_rows(2, 0)
                routed(1, 1, first=True)
                next_weights(1)
                with dve.Fori(2, NT - 3, 2) as t:
                    for s in range(2):
                        split_rows(t + (s + 1), 1 - s)
                        routed(t + s, s)
                        next_weights(t + s)
                split_rows(NT - 1, 1)
                routed(NT - 2, 0)
                routed(NT - 1, 1)

            @block.tensor
            def _(pe):
                pe.wait_ge(S["pool_consts"], 1)
                flat = chosen[:, :, :].rearrange("p g e -> p (g e)")
                nc.tensor.matmul(bank[0][:, :], before[:, :], flat, start=True, stop=True).then_inc(S["cum_ready"], 1)
                nc.tensor.matmul(bank[1][:, :], ones[:, :], flat, start=True, stop=True).then_inc(S["cum_ready"], 1)
                for g in range(TT):
                    t = nc.tensor.matmul(bank[2][0:E, 0:1], chosen[:, g, :], ones[:, 0:1], start=(g == 0), stop=(g == TT - 1))
                t.then_inc(S["counts_ready"], 1)
                pe.wait_ge(S["count_copied"], 1)
                nc.tensor.matmul(bank[3][0:E, 0:1], before[0:E, 0:E], st[:, 1:2], start=True, stop=True).then_inc(S["starts_ready"], 1)
                pe.wait_ge(S["st_ready"], 1)
                for c in range(QC):
                    t = nc.tensor.matmul(bank[4][:, 2 * c:2 * c + 2], expand[:, c * P:(c + 1) * P], st[:, :], start=True, stop=True)
                t.then_inc(S["spread_ready"], 1)
                pe.wait_ge(S["onehot_ready"], 1)

                def gate_up(cols, s, ws):
                    return three(bank[GU[s]][:, :], lambda a, c: xT16[:, a, c, cols], lambda w, c: gu16[:, ws, w, c, :], KC)

                def transposes(s):
                    for c in range(IC):
                        t = nc.tensor.transpose(bank[HT[s]][:, c * P:(c + 1) * P], hid[:, s, c * P:(c + 1) * P], ident[:, :])
                    return t

                def s_transposes(n, s):
                    pe.wait_ge(S["hid_ready"], n + 1)
                    transposes(s).then_inc(S["hidT_ready"], 1)

                def s_down(n, s, ws):
                    pe.wait_ge(S["hlo_ready"], n + 1)
                    three(bank[DN[s]][:, :], lambda a, c: hT16[:, s, a, c * P:(c + 1) * P], lambda w, c: dn16[:, ws, w, c, :], IC).then_inc(S["down_ready"], 1)

                for h in range(SH):
                    pe.wait_ge(S["b_wlo"], 2 * h + 2)
                    n0 = h * TT
                    if h:
                        pe.wait_ge(S["hid_ready"], n0 - 1)
                    gate_up(slice(0, P), 0, h % 2).then_inc(S["gu_ready"], 1)
                    if h:
                        pe.wait_ge(S["added"], n0 - 1)
                    s_transposes(n0, 0)
                    pe.wait_ge(S["hid_ready"], n0)
                    gate_up(slice(P, 2 * P), 1, h % 2).then_inc(S["gu_ready"], 1)
                    s_down(n0, 0, h % 2)
                    s_transposes(n0 + 1, 1)
                    with pe.Fori(2, TT - 1, 2) as g:
                        for s in range(2):
                            n = g + (n0 + s)
                            pe.wait_ge(S["hid_ready"], n - 1)
                            gate_up(bass.ds((g + s) * P, P), s, h % 2).then_inc(S["gu_ready"], 1)
                            pe.wait_ge(S["added"], n - 1)
                            s_down(n - 1, 1 - s, h % 2)
                            pe.wait_ge(S["hlo_ready"], n - 1)
                            s_transposes(n, s)
                    s_down(n0 + TT - 1, 1, h % 2)

                pe.wait_ge(S["table_loaded"], 16)
                for a in range(2):
                    for c in range(QC):
                        nc.tensor.matmul(bank[6][:, a * NT:(a + 1) * NT], tab[:, c, :, a], onehot[:, c, :], start=(c == 0), stop=(c == QC - 1))
                nc.tensor.matmul(bank[7][0:1, 0:NT], ones[0:E, 0:1], steps[:, 0, :], start=True, stop=True)
                t = nc.tensor.matmul(bank[7][0:1, NT:2 * NT], ones[0:E - 1, 0:1], steps[0:E - 1, 1, :], start=True, stop=True)
                t.then_inc(S["ids_psum"], 1)
                pe.wait_ge(S["tables_ready"], 1)
                pe.wait_ge(S["hhi_ready"], SN)

                def rows_T(t, s, x):
                    pe.wait_ge(S[f"gathered{x}"], (t - x) * (16 // XG) + 16)
                    if not (isinstance(t, int) and t < 2):
                        pe.wait_ge(S["xg_lo"], t - 1)
                    for c in range(KC):
                        last = nc.tensor.transpose(bank[XB[s]][:, c * P:(c + 1) * P], xg[:, x, c * P:(c + 1) * P], ident[:, :])
                    last.then_inc(S["xgT_ready"], 1)

                def expert_of(t):
                    return pe.value_load(tile_info[0:1, 0, bass.ds(t, 1)] if not isinstance(t, int) else tile_info[0:1, 0, t:t + 1], min_val=0, max_val=E - 1)

                def gate_up_of(t, s):
                    e = expert_of(t)
                    pe.wait_ge(S["b_wlo"], 2 * e + (2 * SH + 2))
                    pe.wait_ge(S["xg_lo"], t + 1)
                    if not (isinstance(t, int) and t < 2):
                        pe.wait_ge(S["b_hid"], t - 1)
                    w_slot = (e + SH) % 2
                    three(bank[GU[s]][:, :], lambda a, c: xgT[:, s, a, c, :],
                          lambda w, c: gu16[:, bass.ds(w_slot, 1), w, c, :].rearrange("p a n -> p (a n)"), KC).then_inc(S["b_gu"], 1)

                def down_of(t, s):
                    w_slot = (expert_of(t) + SH) % 2
                    pe.wait_ge(S["b_hlo"], t + 1)
                    if not (isinstance(t, int) and t < 2):
                        pe.wait_ge(S["y_ready"], t - 1)
                    three(bank[DN[s]][:, :], lambda a, c: hT16[:, s, a, c * P:(c + 1) * P],
                          lambda w, c: dn16[:, bass.ds(w_slot, 1), w, c, :].rearrange("p a n -> p (a n)"), IC).then_inc(S["b_down"], 1)

                def hidden_T(t, s):
                    pe.wait_ge(S["b_hid"], t + 1)
                    if not (isinstance(t, int) and t < 2):
                        pe.wait_ge(S["b_hlo"], t - 1)
                    transposes(s).then_inc(S["b_hidT"], 1)

                rows_T(0, 0, 0)
                rows_T(1, 1, 1)
                gate_up_of(0, 0)
                hidden_T(0, 0)
                rows_T(2, 0, 2)
                gate_up_of(1, 1)
                down_of(0, 0)
                hidden_T(1, 1)
                with pe.Fori(2, NT - 5, 4) as t:
                    for i in range(4):
                        s = i % 2
                        rows_T(t + (i + 1), 1 - s, (i + 3) % 4)
                        gate_up_of(t + i, s)
                        down_of(t + (i - 1), 1 - s)
                        hidden_T(t + i, s)
                rows_T(NT - 1, 1, 3)
                gate_up_of(NT - 2, 0)
                down_of(NT - 3, 1)
                hidden_T(NT - 2, 0)
                gate_up_of(NT - 1, 1)
                down_of(NT - 2, 0)
                hidden_T(NT - 1, 1)
                down_of(NT - 1, 1)


_INS = ["x", "ctx_512", "L0_xattn_Wq", "L0_xattn_Wk", "L0_xattn_gamma_raw", "L0_ffn_router_w", "L0_ffn_router_bias",
        "L0_ffn_w_gate", "L0_ffn_w_up", "L0_ffn_w_down", "L0_ffn_sw_gate", "L0_ffn_sw_up", "L0_ffn_sw_down"]
_OUTS = [((4 * 512 + 128, 512), "float32")]


def kernel(**inputs):
    import numpy as _np
    import concourse.bacc as _bacc
    from concourse import mybir as _mybir
    from concourse.bass_utils import run_bass_kernel_spmd as _run

    nc = _bacc.Bacc("TRN2", target_bir_lowering=False, num_devices=1)
    arrays, args = {}, []
    for name in _INS:
        a = _np.ascontiguousarray(inputs[name])
        a = a.reshape(a.shape or (1,))
        arrays[f"in_{name}_dram"] = a
        args.append(nc.dram_tensor(f"in_{name}_dram", a.shape, _mybir.dt.from_np(a.dtype), kind="ExternalInput").ap())
    for i, (shape, dtype) in enumerate(_OUTS):
        dt = _mybir.dt.from_np(_np.dtype(dtype))
        args.append(nc.dram_tensor(f"out_{i}_dram", shape, dt, kind="ExternalOutput").ap())
    xattn_moe_kernel(nc, *args)
    r = _run(nc, [arrays], core_ids=[0])
    return _np.asarray(r.results[0]["out_0_dram"])[:4 * 512].reshape(4, 512, 512)
```

```python
from contextlib import ExitStack

import numpy as np

import concourse.bass as bass
from concourse import mybir

F32 = mybir.dt.float32
F16 = mybir.dt.float16
ALU = mybir.AluOpType
I32 = mybir.dt.int32
ACT = mybir.ActivationFunctionType
AX = mybir.AxisListType

P = 128
HEADS = 4
TOP_K_RATIO = 0.3
EPS = 1e-5
GROUPS, TOP_GROUPS, TOP_EXPERTS = 8, 4, 8
ROUTED_SCALE = 2.5
NARROWINGS = 10
BISECTIONS = 26
LOWEST = -3.0e38
W_SCALE = 256.0


class Chain:

    def __init__(self, engine, sem, base=0):
        self.engine, self.sem, self.base, self.n = engine, sem, base, 0

    def done(self, instruction):
        self.n += 1
        instruction.then_inc(self.sem, 1)

    def settle(self):
        self.engine.wait_ge(self.sem, self.base + self.n)

    def step(self, instruction):
        self.done(instruction)
        self.settle()


def xattn_moe_kernel(nc, x, ctx_in, Wq, Wk, gamma_raw, router_w, router_bias, w_gate, w_up, w_down,
                     sw_gate, sw_up, sw_down, out):
    B, N, H = x.shape
    D = ctx_in.shape[2]
    E, _, I = w_gate.shape
    SI = sw_gate.shape[1]
    RT = N // P
    KC = H // P
    IC = I // P
    TT = B * RT
    SH = SI // I
    EG = E // GROUPS
    KEEP = max(1, int(N * TOP_K_RATIO))
    LEAST = TT * TOP_EXPERTS
    PLAIN = LEAST + 2
    SKIP = 8
    NT = LEAST + E + 4
    XG = 4
    DVE_TILES = RT // 2
    DS = 4
    PIECES = 3
    QC = E * TT // P
    SIM_SCALE = 1.0 / (float(np.sqrt(np.float32(D // HEADS))) * HEADS)
    assert D == P and N == 512 and H == 512 and IC == 2

    with ExitStack() as stack:
        def sb(name, shape, dt=F32):
            return stack.enter_context(nc.sbuf_tensor(name, shape, dt))

        def sem(name):
            return stack.enter_context(nc.semaphore(name))

        bank = [stack.enter_context(nc.psum_tensor(f"bank{i}", [P, 512], F32)) for i in range(8)]

        xT16 = sb("xT16", [P, 2, KC, TT * P], F16)
        route = sb("route", [P, TT, E])
        acc = sb("acc", [P, TT, H])
        before = sb("before", [P, P])
        ones = sb("ones", [P, P])
        slot_base = sb("slot_base", [P, E], I32)
        slot_basef = sb("slot_basef", [P, E])
        row_id = sb("row_id", [P, TT], I32)
        row_idf = sb("row_idf", [P, TT])
        trash = sb("trash", [P, 1], I32)
        trashf = sb("trashf", [P, 1])
        tile_no = sb("tile_no", [P, NT], I32)
        tile_nof = sb("tile_nof", [P, NT])
        j_of = sb("j_of", [P, 1], I32)
        j_off = sb("j_off", [P, 1])
        expand = sb("expand", [E, TT * E])
        chosen = sb("chosen", [P, TT, E])
        ident = sb("ident", [P, P])
        xrows = nc.dram_tensor("xrows", [TT * P + P, H], F32).ap()
        table = nc.dram_tensor("table", [E * TT * P, 2], F32).ap()

        SEMS_B = ("cum_ready keys_ready records_ready scattered table_loaded counts_ready count_copied starts_ready "
                  "st_ready spread_ready onehot_ready ids_psum ids_copied tables_ready out_stored "
                  "b_wload b_whi b_wlo gathered0 gathered1 gathered2 gathered3 xgT_ready xg_hi xg_lo "
                  "b_gu b_silu b_hid b_hidT b_hhi b_hlo b_down y_ready added_rows pchain echain")

        names = ("consts ident_zero small_loaded ctx_loaded x_loaded wT_ready wT_copied ctxT_ready hT_ready "
                 "qk_ready qk_copied sim_ready sim_copied dve_chain act_chain pool_chain gamma_ready var_ready sqrt_ready "
                 "coef_ready base_ready sig_ready adj_ready adjT_ready adjT_used mid_ready act_counted few_ready few_summed fallback0 fallback1 fallback2 fallback3 xn_ready xnT_ready xT32_ready "
                 "xhi_ready xlo_ready logits_ready scores_ready routed wload0 wload1 whi_ready wlo_ready gu_ready "
                 "silu_ready hid_ready hidT_ready hhi_ready hlo_ready down_ready added stored "
                 "rows_stored zeroed pool_consts "+SEMS_B).split()
        S = {n: sem(n) for n in names}

        phase = stack.enter_context(ExitStack())

        def sb(name, shape, dt=F32):
            return phase.enter_context(nc.sbuf_tensor(name, shape, dt))

        zeros = sb("zeros", [P, 2 * E * TT])
        w_qk = sb("w_qk", [P, 2, D])
        w_qkT = sb("w_qkT", [P, 2, D])
        gcol = sb("gcol", [P, 4])
        rw = sb("rw", [P, KC, E])
        bias = sb("bias", [P, E])
        ctx_sb = sb("ctx_sb", [P, RT, D])
        x_sb = sb("x_sb", [P, RT, H])
        base = sb("base", [P, RT, H])
        hT = sb("hT", [P, N])
        qT = sb("qT", [P, N])
        kT = sb("kT", [P, N])
        sim = sb("sim", [P, RT, N])
        adj = sb("adj", [P, RT, N])
        under = sb("under", [P, RT, N])
        junk = sb("junk", [P, RT, N], mybir.dt.bfloat16)
        act_junk = sb("act_junk", [P, RT, N], mybir.dt.bfloat16)
        tmp = sb("tmp", [P, RT, N])
        xn = sb("xn", [P, RT, H])
        xT32 = sb("xT32", [P, RT, KC, P])
        st6 = sb("st6", [P, RT, 6])
        mv = sb("mv", [P, RT, 2])
        ve = sb("ve", [P, RT])
        sd = sb("sd", [P, RT])
        rs = sb("rs", [P, RT])
        nt = sb("nt", [P, RT])
        nt2 = sb("nt2", [P, RT])
        coefA = sb("coefA", [P, RT])
        coefB = sb("coefB", [P, RT])
        mx = sb("mx", [P, RT])
        rng = sb("rng", [P, RT])
        lo = sb("lo", [P, RT])
        mid = sb("mid", [P, RT])
        below = sb("below", [P, RT])
        cnt = sb("cnt", [P, RT])
        act_cnt = sb("act_cnt", [P, RT])
        dlt = sb("dlt", [P, RT])
        rank = sb("rank", [P, RT])
        top8 = sb("top8", [P, RT, 8])
        one_to_8 = sb("one_to_8", [P, 8])
        one_to_8i = sb("one_to_8i", [P, 8], I32)
        at_rank = sb("at_rank", [P, RT, 8])
        few = sb("few", [P, RT])
        ones_col = sb("ones_col", [P, 1])
        missed = sb("missed", [1, 1])
        missed_i = sb("missed_i", [1, 1], I32)
        scores = sb("scores", [P, RT, E])
        sg = sb("sg", [P, RT, E])
        pmx = sb("pmx", [P, RT, GROUPS, 2])
        pmn = sb("pmn", [P, RT, GROUPS, 2])
        t1 = sb("t1", [P, RT, GROUPS])
        t2 = sb("t2", [P, RT, GROUPS])
        t3 = sb("t3", [P, RT, GROUPS])
        gs = sb("gs", [P, RT, GROUPS + TOP_GROUPS])
        g8 = sb("g8", [P, RT, 8])
        gtaken = sb("gtaken", [P, RT, GROUPS + TOP_GROUPS])
        gkeep = sb("gkeep", [P, RT, GROUPS])
        masked = sb("masked", [P, RT, E])
        e8 = sb("e8", [P, RT, 8])
        etaken = sb("etaken", [P, RT, E])
        wsel = sb("wsel", [P, RT, E])
        wsum = sb("wsum", [P, RT])
        def _sl(b, i):
            return bass.ds(b * (RT * P) + i * P, P)

        def store_rows(sp, b):
            sp.wait_ge(S["xn_ready"], b + 1)
            sp.dma_start(xrows[b * N:(b + 1) * N, :].rearrange("(i p) h -> p i h", p=P), xn[:, :, :]).then_inc(S["rows_stored"], 16)

        with nc.Block() as block:
            @block.sync
            def _(sp):
                for i, w in enumerate((Wq, Wk)):
                    sp.dma_start(w_qk[:, i, :], w).then_inc(S["small_loaded"], 16)
                sp.dma_start(gcol[:, 0:1], gamma_raw.partition_broadcast(P)).then_inc(S["small_loaded"], 16)
                sp.dma_start(rw[:, :, :], router_w.rearrange("(k p) e -> p k e", p=P)).then_inc(S["small_loaded"], 16)
                sp.dma_start(bias[:, :], router_bias.partition_broadcast(P)).then_inc(S["small_loaded"], 16)
                sp.wait_ge(S["consts"], 3)
                sp.dma_start(xrows[TT * P:, :], zeros[:, 0:H]).then_inc(S["rows_stored"], 16)
                sp.dma_start(out[TT * P:, :], zeros[:, 0:H]).then_inc(S["zeroed"], 16)
                sp.dma_start(table.rearrange("(p s) a -> p (s a)", p=P), zeros[:, :]).then_inc(S["zeroed"], 16)
                for b in range(B):
                    sp.wait_ge(S["ctxT_ready"], b)
                    sp.dma_start(ctx_sb[:, :, :], ctx_in.rearrange("b (i p) d -> b p i d", p=P)[bass.ds(b, 1)].rearrange("b p i d -> (b p) i d")).then_inc(S["ctx_loaded"], 16)
                    sp.wait_ge(S["base_ready"], b * RT)
                    sp.dma_start(x_sb[:, :, :], x.rearrange("b (i p) h -> b p i h", p=P)[bass.ds(b, 1)].rearrange("b p i h -> (b p) i h")).then_inc(S["x_loaded"], 16)
                    if b >= 1:
                        store_rows(sp, b - 1)
                store_rows(sp, B - 1)
                sp.wait_ge(S["rows_stored"], 16 * (B + 1))
                sp.wait_ge(S["zeroed"], 32)

            @block.gpsimd
            def _(pool):
                nc.gpsimd.memset(ident[:, :], 0.0).then_inc(S["ident_zero"], 1)
                pool.wait_ge(S["ident_zero"], 1)
                nc.gpsimd.affine_select(out=ident[:, :], in_=ident[:, :], compare_op=ALU.not_equal, fill=1.0,
                                        base=0, pattern=[[-1, P]], channel_multiplier=1).then_inc(S["consts"], 1)
                nc.gpsimd.memset(zeros[:, :], 0.0).then_inc(S["consts"], 1)
                nc.gpsimd.memset(gs[:, :, GROUPS:], LOWEST).then_inc(S["consts"], 1)
                nc.gpsimd.memset(ones_col[:, :], 1.0).then_inc(S["consts"], 1)
                nc.gpsimd.iota(one_to_8i[:, :], [[1, 8]], base=1, channel_multiplier=0).then_inc(S["consts"], 1)
                ch = Chain(pool, S["echain"])
                ch.done(nc.gpsimd.memset(ones[:, :], 1.0))
                ch.done(nc.gpsimd.memset(before[:, :], 1.0))
                ch.done(nc.gpsimd.memset(expand[:, :], 1.0))
                ch.done(nc.gpsimd.iota(slot_base[:, :], [[TT * P, E]], base=1, channel_multiplier=0))
                ch.done(nc.gpsimd.iota(row_id[:, :], [[P, TT]], base=1, channel_multiplier=1))
                ch.done(nc.gpsimd.iota(trash[:, :], [[0, 1]], base=TT * P + 1, channel_multiplier=1))
                ch.done(nc.gpsimd.iota(tile_no[:, :], [[1, NT]], base=0, channel_multiplier=0))
                ch.done(nc.gpsimd.iota(j_of[:, :], [[0, 1]], base=0, channel_multiplier=1))
                ch.settle()
                ch.done(nc.gpsimd.affine_select(out=before[:, :], in_=before[:, :], compare_op=ALU.is_ge, fill=0.0, base=-1,
                                         pattern=[[1, P]], channel_multiplier=-1))
                ch.step(nc.gpsimd.affine_select(out=expand[:, :], in_=expand[:, :], compare_op=ALU.is_ge, fill=0.0, base=0,
                                         pattern=[[1, TT * E]], channel_multiplier=-TT))
                nc.gpsimd.affine_select(out=expand[:, :], in_=expand[:, :], compare_op=ALU.is_ge, fill=0.0, base=TT - 1,
                                 pattern=[[-1, TT * E]], channel_multiplier=TT).then_inc(S["pool_consts"], 1)
                for b in range(B):
                    pool.wait_ge(S["coef_ready"], b + 1)
                    pool.wait_ge(S["x_loaded"], b * 16 + 16)
                    pool.wait_ge(S["xn_ready"], b)
                    for i in range(RT):
                        nc.gpsimd.tensor_scalar(base[:, i, :], x_sb[:, i, :], coefA[:, i:i + 1], coefB[:, i:i + 1],
                                                ALU.mult, ALU.add).then_inc(S["base_ready"], 1)

            @block.tensor
            def _(pe):
                pe.wait_ge(S["consts"], 1)
                pe.wait_ge(S["small_loaded"], 5 * 16)
                for i in range(2):
                    nc.tensor.transpose(bank[1][:, i * D:(i + 1) * D], w_qk[:, i, :], ident[:, :]).then_inc(S["wT_ready"], 1)
                pe.wait_ge(S["wT_copied"], 1)

                def queries_keys(b):
                    pe.wait_ge(S["ctx_loaded"], b * 16 + 16)
                    for i in range(RT):
                        t = nc.tensor.transpose(bank[0][:, i * P:(i + 1) * P], ctx_sb[:, i, :], ident[:, :])
                    t.then_inc(S["ctxT_ready"], 1)
                    pe.wait_ge(S["hT_ready"], b + 1)
                    if b >= 2:
                        pe.wait_ge(S["xT32_ready"], RT * (b - 1))
                    for i in range(2):
                        nc.tensor.matmul(bank[1 + i][:, :], w_qkT[:, i, :], hT[:, :], start=True, stop=True).then_inc(S["qk_ready"], 1)

                def similarities(b):
                    pe.wait_ge(S["qk_copied"], 2 * b + 2)
                    if b >= 1:
                        pe.wait_ge(S["adjT_used"], RT * b)
                    for i in range(RT):
                        nc.tensor.matmul(bank[3 + i][:, :], qT[:, i * P:(i + 1) * P], kT[:, :], start=True, stop=True).then_inc(S["sim_ready"], 1)

                queries_keys(0)
                similarities(0)
                pe.wait_ge(S["consts"], 5)
                for b in range(B):
                    if b + 1 < B:
                        queries_keys(b + 1)
                    pe.wait_ge(S["few_ready"], b + 1)
                    nc.tensor.matmul(bank[7][0:1, P:P + RT], ones_col[:, :], few[:, :], start=True, stop=True).then_inc(S["few_summed"], 1)
                    pe.wait_ge(S["sim_copied"], RT * b + RT)
                    pe.wait_ge(S["adj_ready"], RT * b + RT)
                    for i in range(RT):
                        for j in range(RT):
                            t = nc.tensor.transpose(bank[3 + i][:, j * P:(j + 1) * P], adj[:, j, i * P:(i + 1) * P], ident[:, :])
                        t.then_inc(S["adjT_ready"], 1)
                    if b + 1 < B:
                        similarities(b + 1)
                    pe.wait_ge(S["xn_ready"], b + 1)
                    for i in range(RT):
                        if i >= 2:
                            pe.wait_ge(S["xT32_ready"], RT * b + i - 1)
                        for k in range(KC):
                            t = nc.tensor.transpose(bank[1 + i % 2][:, k * P:(k + 1) * P], xn[:, i, k * P:(k + 1) * P], ident[:, :])
                        t.then_inc(S["xnT_ready"], 1)
                    if b >= 1:
                        pe.wait_ge(S["scores_ready"], b)
                    for i in range(RT):
                        pe.wait_ge(S["xT32_ready"], RT * b + i + 1)
                        for k in range(KC):
                            t = nc.tensor.matmul(bank[7][:, i * E:(i + 1) * E], xT32[:, i, k, :], rw[:, k, :],
                                                 start=(k == 0), stop=(k == KC - 1))
                    t.then_inc(S["logits_ready"], 1)

            @block.scalar
            def _(act):
                act.wait_ge(S["small_loaded"], 5 * 16)
                nc.scalar.activation(gcol[:, 1:2], gcol[:, 0:1], ACT.Sigmoid).then_inc(S["gamma_ready"], 1)

                def root():
                    roots = act_roots[0] = act_roots[0] + 1
                    act.wait_ge(S["var_ready"], roots)
                    nc.scalar.activation(sd[:, :], ve[:, :], ACT.Sqrt).then_inc(S["sqrt_ready"], 1)

                def queries_keys(b):
                    act.wait_ge(S["ctxT_ready"], b + 1)
                    nc.scalar.copy(hT[:, :], bank[0][:, :]).then_inc(S["hT_ready"], 1)
                    for i, t in enumerate((qT, kT)):
                        act.wait_ge(S["qk_ready"], 2 * b + i + 1)
                        nc.scalar.copy(t[:, :], bank[1 + i][:, :]).then_inc(S["qk_copied"], 1)

                def similarities(b):
                    if b >= 1:
                        act.wait_ge(S["adj_ready"], RT * b)
                    for i in range(RT):
                        act.wait_ge(S["sim_ready"], RT * b + i + 1)
                        nc.scalar.mul(sim[:, i, :], bank[3 + i][:, :], SIM_SCALE).then_inc(S["sim_copied"], 1)
                    act.wait_ge(S["sim_copied"], RT * b + RT)
                    if b >= 1:
                        act.wait_ge(S["adjT_used"], RT * b)
                    nc.scalar.activation(adj[:, :, :], sim[:, :, :], ACT.Sigmoid).then_inc(S["sig_ready"], 1)

                act_roots = [0]
                queries_keys(0)
                root()
                similarities(0)
                for b in range(B):
                    with act.Fori(0, NARROWINGS) as it:
                        act.wait_ge(S["mid_ready"], it + (b * (NARROWINGS + 1) + 1))
                        for i in range(DVE_TILES, RT):
                            nc.scalar.activation(act_junk[:, i - DVE_TILES, :], sim[:, i, :], ACT.Sign, bias=mid[:, i:i + 1], scale=-1.0,
                                                 accum_out=act_cnt[:, i:i + 1]).then_inc(S["act_counted"], 1)
                    if b + 1 < B:
                        queries_keys(b + 1)
                    root()
                    if b + 1 < B:
                        root()
                    for i in range(RT):
                        act.wait_ge(S["xT32_ready"], RT * b + i + 1)
                        nc.scalar.copy(xT16[:, 0, :, _sl(b, i)], xT32[:, i, :, :]).then_inc(S["xhi_ready"], 1)
                    act.wait_ge(S["logits_ready"], b + 1)
                    nc.scalar.activation(scores[:, :, :], bank[7][:, 0:RT * E].rearrange("p (i e) -> p i e", e=E),
                                         ACT.Sigmoid).then_inc(S["scores_ready"], 1)
                    if b + 1 < B:
                        similarities(b + 1)

            @block.vector
            def _(dve):
                dve.wait_ge(S["wT_ready"], 2)
                nc.vector.tensor_copy(w_qkT[:, :, :], bank[1][:, 0:2 * D].rearrange("p (a d) -> p a d", a=2)).then_inc(S["wT_copied"], 1)
                dve.wait_ge(S["gamma_ready"], 1)
                ch = Chain(dve, S["dve_chain"])
                ch.done(nc.vector.tensor_scalar(gcol[:, 2:3], gcol[:, 1:2], -1.0, 1.0, ALU.mult, ALU.add))
                ch.step(nc.vector.tensor_scalar(gcol[:, 3:4], gcol[:, 1:2], 0.5, None, ALU.mult))
                dve.wait_ge(S["consts"], 5)
                ch.step(nc.vector.tensor_copy(one_to_8[:, :], one_to_8i[:, :]))
                v = nc.vector

                def variances():
                    for i in range(RT):
                        ch.done(v.bn_aggr(mv[:, i, :], st6[:, i, :]))
                    ch.settle()
                    v.tensor_scalar(ve[:, :], mv[:, :, 1], EPS, None, ALU.add).then_inc(S["var_ready"], 1)

                def inverse_std(nth):
                    dve.wait_ge(S["var_ready"], nth)
                    dve.wait_ge(S["sqrt_ready"], nth)
                    ch.step(v.reciprocal(rs[:, :], sd[:, :]))
                    ch.step(v.tensor_tensor(nt[:, :], rs[:, :], rs[:, :], ALU.mult))
                    ch.step(v.tensor_tensor(nt2[:, :], nt[:, :], ve[:, :], ALU.mult))
                    ch.step(v.tensor_scalar(nt[:, :], nt2[:, :], -0.5, 1.5, ALU.mult, ALU.add))
                    ch.step(v.tensor_tensor(rs[:, :], rs[:, :], nt[:, :], ALU.mult))

                def x_variances(b):
                    dve.wait_ge(S["x_loaded"], b * 16 + 16)
                    for i in range(RT):
                        ch.done(v.bn_stats(st6[:, i, :], x_sb[:, i, :]))
                    ch.settle()
                    variances()

                def coefficients(b):
                    inverse_std(2 * b + 1)
                    ch.step(v.tensor_scalar(nt[:, :], rs[:, :], gcol[:, 2:3], None, ALU.mult))
                    ch.done(v.tensor_scalar(coefA[:, :], nt[:, :], 1.0, None, ALU.add))
                    v.scalar_tensor_tensor(coefB[:, :], nt[:, :], -1.0, mv[:, :, 0], ALU.mult, ALU.mult).then_inc(S["coef_ready"], 1)

                def batch(b):
                    dve.wait_ge(S["sim_copied"], RT * b + RT)
                    ch.done(v.tensor_reduce(mx[:, :], sim[:, :, :], AX.X, ALU.max))
                    ch.step(v.tensor_reduce(lo[:, :], sim[:, :, :], AX.X, ALU.min))
                    ch.step(v.tensor_tensor(rng[:, :], mx[:, :], lo[:, :], ALU.subtract))
                    ch.done(v.tensor_scalar(rng[:, :], rng[:, :], 0.5, None, ALU.mult))
                    ch.step(v.tensor_tensor(mid[:, :], mx[:, :], lo[:, :], ALU.add))
                    v.tensor_scalar(mid[:, :], mid[:, :], 0.5, None, ALU.mult).then_inc(S["mid_ready"], 1)
                    per = 6
                    mids = b * (NARROWINGS + 1)
                    with dve.Fori(0, NARROWINGS) as it:
                        inner = Chain(dve, S["dve_chain"], it * per + (ch.base + ch.n))
                        dve.wait_ge(S["mid_ready"], it + (mids + 1))
                        inner.done(v.scalar_tensor_tensor(below[:, :], rng[:, :], -0.5, mid[:, :], ALU.mult, ALU.add))
                        for i in range(DVE_TILES):
                            inner.done(v.tensor_scalar(junk[:, i, :], sim[:, i, :], mid[:, i:i + 1], 0.0, ALU.is_ge, ALU.add,
                                                       accum_out=cnt[:, i:i + 1]))
                        inner.settle()
                        inner.done(v.scalar_tensor_tensor(dlt[:, 0:DVE_TILES], cnt[:, 0:DVE_TILES], KEEP - 0.5, rng[:, 0:DVE_TILES], ALU.is_ge, ALU.mult))
                        dve.wait_ge(S["act_counted"], (it + (b * NARROWINGS + 1)) * (RT - DVE_TILES))
                        inner.step(v.scalar_tensor_tensor(dlt[:, DVE_TILES:], act_cnt[:, DVE_TILES:], N - 2 * KEEP + 1.0, rng[:, DVE_TILES:], ALU.is_le, ALU.mult))
                        v.tensor_tensor(mid[:, :], below[:, :], dlt[:, :], ALU.add).then_inc(S["mid_ready"], 1)
                        inner.step(v.tensor_scalar(rng[:, :], rng[:, :], 0.5, None, ALU.mult))
                        assert inner.n == per
                    ch.n += per * NARROWINGS
                    dve.wait_ge(S["mid_ready"], mids + NARROWINGS + 1)
                    ch.step(v.tensor_tensor(mid[:, :], mid[:, :], rng[:, :], ALU.add))
                    for i in range(RT):
                        ch.done(v.tensor_scalar(junk[:, i, :], sim[:, i, :], mid[:, i:i + 1], 0.0, ALU.is_ge, ALU.add,
                                                accum_out=cnt[:, i:i + 1]))
                    ch.settle()
                    for i in range(RT):
                        ch.done(v.scalar_tensor_tensor(under[:, i, :], junk[:, i, :], LOWEST, sim[:, i, :], ALU.mult, ALU.add))
                    ch.settle()
                    for i in range(RT):
                        ch.done(v.max(top8[:, i, :], under[:, i, :]))
                    ch.step(v.tensor_scalar(rank[:, :], cnt[:, :], -1.0, float(KEEP), ALU.mult, ALU.add))
                    ch.step(v.tensor_tensor(at_rank[:, :, :], one_to_8[:, :].unsqueeze(1).to_broadcast([P, RT, 8]),
                                            rank[:, :].unsqueeze(2).to_broadcast([P, RT, 8]), ALU.is_equal))
                    v.tensor_reduce(few[:, :], at_rank[:, :, :], AX.X, ALU.add).then_inc(S["few_ready"], 1)
                    ch.step(v.tensor_tensor(top8[:, :, :], top8[:, :, :], at_rank[:, :, :], ALU.mult))
                    ch.step(v.tensor_reduce(lo[:, :], top8[:, :, :], AX.X, ALU.add))
                    dve.wait_ge(S["few_summed"], b + 1)
                    ch.step(v.tensor_reduce(missed[:, :], bank[7][0:1, P:P + RT], AX.X, ALU.add))
                    ch.step(v.tensor_scalar(missed_i[:, :], missed[:, :], -1.0, float(N), ALU.mult, ALU.add))
                    with dve.If(dve.value_load(missed_i[0:1, 0:1], min_val=0, max_val=N) > 0):
                        own = Chain(dve, S[f"fallback{b}"])
                        own.step(v.tensor_reduce(lo[:, :], sim[:, :, :], AX.X, ALU.min))
                        own.step(v.tensor_tensor(rng[:, :], mx[:, :], lo[:, :], ALU.subtract))
                        own.step(v.tensor_scalar(rng[:, :], rng[:, :], 0.5, None, ALU.mult))
                        per = RT + 4
                        with dve.Fori(0, BISECTIONS) as it:
                            inner = Chain(dve, S[f"fallback{b}"], it * per + own.n)
                            inner.step(v.tensor_tensor(mid[:, :], lo[:, :], rng[:, :], ALU.add))
                            for i in range(RT):
                                inner.done(v.tensor_scalar(junk[:, i, :], sim[:, i, :], mid[:, i:i + 1], 0.0, ALU.is_ge, ALU.add,
                                                           accum_out=cnt[:, i:i + 1]))
                            inner.settle()
                            inner.step(v.scalar_tensor_tensor(dlt[:, :], cnt[:, :], KEEP - 0.5, rng[:, :], ALU.is_ge, ALU.mult))
                            inner.done(v.tensor_tensor(lo[:, :], lo[:, :], dlt[:, :], ALU.add))
                            inner.step(v.tensor_scalar(rng[:, :], rng[:, :], 0.5, None, ALU.mult))
                            assert inner.n == per

                    dve.wait_ge(S["sig_ready"], b + 1)
                    for i in range(RT):
                        v.scalar_tensor_tensor(adj[:, i, :], sim[:, i, :], lo[:, i:i + 1], adj[:, i, :],
                                               ALU.is_ge, ALU.mult).then_inc(S["adj_ready"], 1)
                    dve.wait_ge(S["adj_ready"], RT * b + RT)
                    dve.wait_ge(S["base_ready"], RT * b + RT)
                    for i in range(RT):
                        dve.wait_ge(S["adjT_ready"], RT * b + i + 1)
                        v.tensor_tensor(tmp[:, i, :], adj[:, i, :], bank[3 + i][:, :], ALU.add).then_inc(S["adjT_used"], 1)
                    dve.wait_ge(S["adjT_used"], RT * b + RT)
                    for i in range(RT):
                        ch.done(v.scalar_tensor_tensor(acc[:, b * RT + i, :], tmp[:, i, :], gcol[:, 3:4], base[:, i, :], ALU.mult, ALU.add))
                    ch.settle()
                    for i in range(RT):
                        ch.done(v.bn_stats(st6[:, i, :], acc[:, b * RT + i, :]))
                    ch.settle()
                    variances()
                    inverse_std(2 * b + 2)
                    if b >= 1:
                        dve.wait_ge(S["rows_stored"], 16 * b + 16)
                    for i in range(RT):
                        t = v.tensor_scalar(xn[:, i, :], acc[:, b * RT + i, :], mv[:, i, 0:1], rs[:, i:i + 1],
                                            ALU.subtract, ALU.mult)
                        if i < RT - 1:
                            ch.done(t)
                    t.then_inc(S["xn_ready"], 1)
                    dve.wait_ge(S["xn_ready"], b + 1)
                    if b + 1 < B:
                        x_variances(b + 1)

                    def low_part(i):
                        dve.wait_ge(S["xhi_ready"], RT * b + i + 1)
                        v.tensor_tensor(xT16[:, 1, :, _sl(b, i)], xT32[:, i, :, :], xT16[:, 0, :, _sl(b, i)],
                                        ALU.subtract).then_inc(S["xlo_ready"], 1)

                    for i in range(RT):
                        dve.wait_ge(S["xnT_ready"], RT * b + i + 1)
                        v.tensor_copy(xT32[:, i, :, :], bank[1 + i % 2][:, :].rearrange("p (k t) -> p k t", k=KC)).then_inc(S["xT32_ready"], 1)
                        if i:
                            low_part(i - 1)
                    low_part(RT - 1)
                    if b + 1 < B:
                        coefficients(b + 1)

                    dve.wait_ge(S["scores_ready"], b + 1)
                    ch.step(v.tensor_tensor(sg[:, :, :], scores[:, :, :], bias[:, :].unsqueeze(1).to_broadcast([P, RT, E]), ALU.add))
                    q = sg[:, :, :].rearrange("p i (g a c) -> p i g a c", a=2, c=2)
                    for c in range(RT):
                        ch.done(v.tensor_tensor(pmx[:, c, :, :], q[:, c, :, :, 0], q[:, c, :, :, 1], ALU.max))
                        ch.done(v.tensor_tensor(pmn[:, c, :, :], q[:, c, :, :, 0], q[:, c, :, :, 1], ALU.min))
                    ch.settle()
                    ch.done(v.tensor_tensor(t1[:, :, :], pmx[:, :, :, 0], pmx[:, :, :, 1], ALU.max))
                    ch.done(v.tensor_tensor(t2[:, :, :], pmx[:, :, :, 0], pmx[:, :, :, 1], ALU.min))
                    ch.step(v.tensor_tensor(t3[:, :, :], pmn[:, :, :, 0], pmn[:, :, :, 1], ALU.max))
                    ch.step(v.tensor_tensor(t2[:, :, :], t2[:, :, :], t3[:, :, :], ALU.max))
                    ch.step(v.tensor_tensor(gs[:, :, 0:GROUPS], t1[:, :, :], t2[:, :, :], ALU.add))
                    for i in range(RT):
                        ch.done(v.max(g8[:, i, :], gs[:, i, 0:GROUPS]))
                    ch.settle()
                    ch.step(v.memset(g8[:, :, TOP_GROUPS:], LOWEST))
                    for i in range(RT):
                        ch.done(v.match_replace(gtaken[:, i, :], g8[:, i, :], gs[:, i, :], LOWEST))
                    ch.settle()
                    ch.step(v.tensor_scalar(gkeep[:, :, :], gtaken[:, :, 0:GROUPS], LOWEST / 2, None, ALU.is_le))
                    for i in range(RT):
                        ch.done(v.tensor_tensor(masked[:, i, :].rearrange("p (g c) -> p g c", c=EG), sg[:, i, :].rearrange("p (g c) -> p g c", c=EG),
                                                gkeep[:, i, :].unsqueeze(2).to_broadcast([P, GROUPS, EG]), ALU.mult))
                    ch.settle()
                    for i in range(RT):
                        ch.done(v.max(e8[:, i, :], masked[:, i, :]))
                    ch.settle()
                    for i in range(RT):
                        ch.done(v.match_replace(etaken[:, i, :], e8[:, i, :], masked[:, i, :], LOWEST))
                    ch.settle()
                    ch.done(v.tensor_scalar(chosen[:, b * RT:(b + 1) * RT, :], etaken[:, :, :], LOWEST / 2, None, ALU.is_le))
                    ch.step(v.scalar_tensor_tensor(wsel[:, :, :], etaken[:, :, :], LOWEST / 2, scores[:, :, :], ALU.is_le, ALU.mult))
                    ch.step(v.tensor_reduce(wsum[:, :], wsel[:, :, :], AX.X, ALU.add))
                    ch.step(v.reciprocal(wsum[:, :], wsum[:, :]))
                    for i in range(RT):
                        t = v.tensor_scalar(route[:, bass.ds(b * RT + i, 1), 0:E].rearrange("p a e -> p (a e)"), wsel[:, i, :], wsum[:, i:i + 1], ROUTED_SCALE, ALU.mult, ALU.mult)
                        if i < RT - 1:
                            ch.done(t)
                    t.then_inc(S["routed"], 1)

                x_variances(0)
                coefficients(0)
                for b in range(B):
                    batch(b)

        phase.close()

        stage_gu = sb("stage_gu", [P, KC, 2, I])
        stage_dn = sb("stage_dn", [P, IC, H])
        gu16 = sb("gu16", [P, 2, 2, KC, 2 * I], F16)
        dn16 = sb("dn16", [P, DS, 2, IC, H], F16)
        silu = sb("silu", [P, 2, I])
        hid = sb("hid", [P, 2, I])
        hT16 = sb("hT16", [P, 2, 2, I], F16)
        xg = sb("xg", [P, XG, H])
        xgT = sb("xgT", [P, 2, 2, KC, P], F16)
        y = sb("y", [P, 2, H])
        carry = sb("carry", [P, 2, TT, E])
        key = sb("key", [P, TT, E])
        key8 = sb("key8", [P, TT, TOP_EXPERTS])
        key8i = sb("key8i", [P, TT, TOP_EXPERTS], I32)
        match = sb("match", [P, RT, TOP_EXPERTS, E])
        record = sb("record", [P, TT, TOP_EXPERTS, 2])
        tab = sb("tab", [P, QC, P, 2])
        n_e = sb("n_e", [E, 1])
        n_i = sb("n_i", [E, 1], I32)
        n_t = sb("n_t", [E, 1], I32)
        st = sb("st", [E, 2])
        spread = sb("spread", [P, QC, 2])
        live = sb("live", [P, QC])
        target = sb("target", [P, QC])
        onehot = sb("onehot", [P, QC, NT])
        steps = sb("steps", [E, 2, NT])
        pad = sb("pad", [P, NT])
        ids = sb("ids", [P, NT])
        ids_i = sb("ids_i", [P, NT], I32)
        wts = sb("wts", [P, NT])
        tile_info = sb("tile_info", [1, 3, NT], I32)
        in_use = sb("in_use", [1, 1])
        results = sb("results", [1, 1], I32)

        GU, HT, DN = (0, 1), (2, 3), (4, 5)
        XB = (6, 7)
        OPEN = (6,) + (2,) * (SH - 1)
        SN = SH * TT

        def gu_slot(n, part, piece):
            if isinstance(n, int):
                return gu16[:, n % 2, part, 2 * piece:2 * piece + 2, :].rearrange("p k n -> p (k n)")
            return gu16[:, bass.ds(n % 2, 1), part, 2 * piece:2 * piece + 2, :].rearrange("p a k n -> p (a k n)")

        def dn_slot(n, part):
            if isinstance(n, int):
                return dn16[:, n % DS, part].rearrange("p k n -> p (k n)")
            return dn16[:, bass.ds(n % DS, 1), part].rearrange("p a k n -> p (a k n)")

        def info_of(engine, what, t):
            at = tile_info[0:1, what, t:t + 1] if isinstance(t, int) else tile_info[0:1, what, bass.ds(t, 1)]
            return engine.value_load(at, min_val=0, max_val=(E - 1, 1, 1)[what])

        def three(out_ap, stationary, moving, chunks):
            parts = [(0, 0), (0, 1), (1, 0)]
            for c in range(chunks):
                for a, w in parts:
                    last = nc.tensor.matmul(out_ap, stationary(a, c), moving(w, c), start=(c == 0 and (a, w) == parts[0]),
                                            stop=(c == chunks - 1 and (a, w) == parts[-1]))
            return last

        with nc.Block() as block:
            @block.sync
            def _(sp):
                def load(n, g, u, d):
                    if not (isinstance(n, int) and n == 0):
                        sp.wait_ge(S["b_wlo"], PIECES * n)
                    sp.dma_start(stage_gu[:, :, 0, :], g.rearrange("(k p) i -> p k i", p=P)).then_inc(S["b_wload"], 16)
                    sp.dma_start(stage_gu[:, :, 1, :], u.rearrange("(k p) i -> p k i", p=P)).then_inc(S["b_wload"], 16)
                    sp.dma_start(stage_dn[:, :, :], d.rearrange("(k p) h -> p k h", p=P)).then_inc(S["b_wload"], 16)

                for h in range(SH):
                    c = slice(h * I, (h + 1) * I)
                    load(h, sw_gate[:, c], sw_up[:, c], sw_down[c, :])
                load(SH, w_gate[0], w_up[0], w_down[0])
                with sp.Fori(0, TT) as g:
                    sp.wait_ge(S["added"], g + ((SH - 1) * TT + 1))
                    sp.dma_start(out[bass.ds(g * P, P), :], acc[:, bass.ds(g, 1), :].rearrange("p a h -> p (a h)")).then_inc(S["out_stored"], 16)
                with sp.Fori(1, E) as e:
                    load(e + SH, *(w[bass.ds(e, 1)].rearrange("a k n -> (a k) n") for w in (w_gate, w_up, w_down)))

            @block.gpsimd
            def _(pool):
                g_ = nc.gpsimd
                for g in range(TT):
                    pool.wait_ge(S["records_ready"], g // RT + 1)
                    if g == 0:
                        pool.wait_ge(S["zeroed"], 32)
                    for k in range(TOP_EXPERTS):
                        g_.indirect_dma_start(table, bass.IndirectOffsetOnAxis(ap=key8i[:, g, k:k + 1], axis=0),
                                              record[:, g, k, :], None).then_inc(S["scattered"], 16)
                pool.wait_ge(S["scattered"], 16 * TT * TOP_EXPERTS)
                g_.dma_start(tab[:, :, :, :].rearrange("p c s a -> p c (s a)"), table.rearrange("(c p s) a -> p c (s a)", p=P, s=P)).then_inc(S["table_loaded"], 16)
                pool.wait_ge(S["tables_ready"], 1)
                pool.wait_ge(S["rows_stored"], 16 * (B + 1))
                pool.wait_ge(S["zeroed"], 32)

                def gather(t):
                    if t >= XG:
                        pool.wait_ge(S["xgT_ready"], t - XG + 1)
                    g_.indirect_dma_start(xg[:, t % XG, :], None, xrows,
                                          bass.IndirectOffsetOnAxis(ap=ids_i[:, t:t + 1], axis=0)).then_inc(S[f"gathered{t % XG}"], 16)

                def scatter(t):
                    pool.wait_ge(S["y_ready"], t + 1)
                    if t >= 1:
                        pool.wait_ge(S["added_rows"], t * 16)
                    g_.indirect_dma_start(out, bass.IndirectOffsetOnAxis(ap=ids_i[:, t:t + 1], axis=0), y[:, t % 2, :], None,
                                          compute_op=ALU.add).then_inc(S["added_rows"], 16)

                for t in range(XG + 1):
                    gather(t)
                pool.wait_ge(S["out_stored"], 16 * TT)
                for t in range(PLAIN - 1):
                    gather(t + XG + 1)
                    scatter(t)
                for group in range(PLAIN, LEAST + E, SKIP):
                    with pool.If(info_of(pool, 2, group) > 0):
                        for t in range(group, min(group + SKIP, LEAST + E)):
                            with pool.If(info_of(pool, 2, t) > 0):
                                gather(t + XG)
                                scatter(t - 1)
                pool.wait_ge(S["added_rows"], pool.value_load(results[0:1, 0:1], min_val=PLAIN - 1, max_val=LEAST + E) * 16)

            @block.scalar
            def _(act):
                a_ = nc.scalar

                def convert(n):
                    act.wait_ge(S["b_wload"], n * 48 + 48)
                    for piece in range(2):
                        a_.mul(gu_slot(n, 0, piece), stage_gu[:, 2 * piece:2 * piece + 2, :, :].rearrange("p k a i -> p (k a i)"),
                               W_SCALE).then_inc(S["b_whi"], 1)
                    a_.mul(dn_slot(n, 0), stage_dn[:, :, :].rearrange("p k h -> p (k h)"), W_SCALE).then_inc(S["b_whi"], 1)

                def shared(n, s, first=False):
                    act.wait_ge(S["gu_ready"], n + 1)
                    if not first:
                        act.wait_ge(S["hid_ready"], n - 1)
                    a_.activation(silu[:, s, :], bank[GU[s]][:, 0:I], ACT.Silu, scale=1.0 / W_SCALE).then_inc(S["silu_ready"], 1)
                    act.wait_ge(S["hidT_ready"], n + 1)
                    if not first:
                        act.wait_ge(S["down_ready"], n - 1)
                    a_.copy(hT16[:, s, 0, :], bank[HT[s]][:, 0:I]).then_inc(S["hhi_ready"], 1)

                convert(0)
                for h in range(SH):
                    for n in range(OPEN[h]):
                        shared(h * TT + n, n % 2, first=(h == 0 and n < 2))
                    if h:
                        act.wait_ge(S["down_ready"], h * TT)
                    convert(h + 1)
                    with act.Fori(OPEN[h], TT - 1, 2) as g:
                        for s in range(2):
                            shared(g + (s + h * TT), s)
                act.wait_ge(S["tables_ready"], 1)

                def split_rows(t, s):
                    act.wait_ge(S["xgT_ready"], t + 1)
                    if not (isinstance(t, int) and t < 2):
                        act.wait_ge(S["b_gu"], t - 1)
                    a_.copy(xgT[:, s, 0, :, :], bank[XB[s]][:, :].rearrange("p (k t) -> p k t", k=KC)).then_inc(S["xg_hi"], 1)

                def gates(t, s):
                    act.wait_ge(S["b_gu"], t + 1)
                    if not (isinstance(t, int) and t < 2):
                        act.wait_ge(S["b_hid"], t - 1)
                    a_.activation(silu[:, s, :], bank[GU[s]][:, 0:I], ACT.Silu, scale=1.0 / W_SCALE).then_inc(S["b_silu"], 1)

                def next_weights(t):
                    with act.If(info_of(act, 1, t) > 0):
                        convert(info_of(act, 0, t) + (SH + 1))

                def hidden(t, s):
                    act.wait_ge(S["b_hidT"], t + 1)
                    if not (isinstance(t, int) and t < 2):
                        act.wait_ge(S["b_down"], t - 1)
                    a_.copy(hT16[:, s, 0, :], bank[HT[s]][:, 0:I]).then_inc(S["b_hhi"], 1)

                def result(t, s):
                    act.wait_ge(S["b_down"], t + 1)
                    if not (isinstance(t, int) and t < 2):
                        act.wait_ge(S["added_rows"], (t - 1) * 16)
                    w = wts[:, t:t + 1] if isinstance(t, int) else wts[:, bass.ds(t, 1)]
                    a_.activation(y[:, s, :], bank[DN[s]][:, :], ACT.Identity, scale=w).then_inc(S["y_ready"], 1)

                split_rows(0, 0)
                split_rows(1, 1)
                for t in range(2):
                    gates(t, t)
                    split_rows(t + 2, t)
                    next_weights(t)
                    hidden(t, t)
                    if t:
                        result(t - 1, 1 - t)
                def step(t, s):
                    gates(t, s)
                    split_rows(t + 2, s)
                    next_weights(t)
                    hidden(t, s)
                    result(t - 1, 1 - s)

                with act.Fori(2, PLAIN - 1, 2) as t:
                    for s in range(2):
                        step(t + s, s)
                with act.Fori(PLAIN, PLAIN + E - SKIP + 1, SKIP) as t:
                    with act.If(info_of(act, 2, t) > 0):
                        for i in range(SKIP):
                            with act.If(info_of(act, 2, t + i) > 0):
                                step(t + i, i % 2)

            @block.vector
            def _(dve):
                v = nc.vector
                ch = Chain(dve, S["pchain"])
                def convert(n):
                    for piece in range(2):
                        dve.wait_ge(S["b_whi"], PIECES * n + (piece + 1))
                        v.scalar_tensor_tensor(gu_slot(n, 1, piece), stage_gu[:, 2 * piece:2 * piece + 2, :, :].rearrange("p k a i -> p (k a i)"),
                                               W_SCALE, gu_slot(n, 0, piece), ALU.mult, ALU.subtract).then_inc(S["b_wlo"], 1)
                    dve.wait_ge(S["b_whi"], PIECES * n + PIECES)
                    v.scalar_tensor_tensor(dn_slot(n, 1), stage_dn[:, :, :].rearrange("p k h -> p (k h)"),
                                           W_SCALE, dn_slot(n, 0), ALU.mult, ALU.subtract).then_inc(S["b_wlo"], 1)

                def add_shared(n, g, s):
                    dve.wait_ge(S["down_ready"], n + 1)
                    a = acc[:, g, :] if isinstance(g, int) else acc[:, bass.ds(g, 1), :].rearrange("p a h -> p (a h)")
                    v.scalar_tensor_tensor(a, bank[DN[s]][:, :], 1.0 / W_SCALE, a, ALU.mult, ALU.add).then_inc(S["added"], 1)

                def shared(n, g, s):
                    dve.wait_ge(S["silu_ready"], n + 1)
                    if not (isinstance(n, int) and n < 2):
                        dve.wait_ge(S["hidT_ready"], n - 1)
                    v.scalar_tensor_tensor(hid[:, s, :], bank[GU[s]][:, I:2 * I], 1.0 / W_SCALE, silu[:, s, :],
                                           ALU.mult, ALU.mult).then_inc(S["hid_ready"], 1)
                    if g is not None:
                        add_shared(n - 1, g, 1 - s)
                    dve.wait_ge(S["hhi_ready"], n + 1)
                    v.tensor_tensor(hT16[:, s, 1, :], bank[HT[s]][:, 0:I], hT16[:, s, 0, :], ALU.subtract).then_inc(S["hlo_ready"], 1)

                def find_keys():
                    dve.wait_ge(S["pool_consts"], 1)
                    ch.done(v.tensor_copy(slot_basef[:, :], slot_base[:, :]))
                    ch.done(v.tensor_copy(row_idf[:, :], row_id[:, :]))
                    ch.done(v.tensor_copy(trashf[:, :], trash[:, :]))
                    ch.done(v.tensor_copy(tile_nof[:, :], tile_no[:, :]))
                    ch.step(v.tensor_scalar(j_of[:, :], j_of[:, :], TT - 1, None, ALU.bitwise_and))
                    ch.step(v.tensor_copy(j_off[:, :], j_of[:, :]))
                    dve.wait_ge(S["cum_ready"], 2)
                    ch.done(v.memset(carry[:, 0, 0:1, :], 0.0))
                    ch.step(v.tensor_copy(carry[:, 0, 1:TT, :], bank[7][:, 0:(TT - 1) * E].rearrange("p (g e) -> p g e", e=E)))
                    cur, d = 0, 1
                    while d < TT:
                        ch.done(v.tensor_copy(carry[:, 1 - cur, 0:d, :], carry[:, cur, 0:d, :]))
                        ch.step(v.tensor_tensor(carry[:, 1 - cur, d:, :], carry[:, cur, d:, :], carry[:, cur, 0:TT - d, :], ALU.add))
                        cur, d = 1 - cur, 2 * d
                    ch.step(v.tensor_tensor(key[:, :, :], carry[:, cur, :, :], bank[6][:, :].rearrange("p (g e) -> p g e", e=E), ALU.add))
                    ch.step(v.tensor_tensor(key[:, :, :], key[:, :, :], slot_basef[:, :].unsqueeze(1).to_broadcast([P, TT, E]), ALU.add))
                    ch.step(v.tensor_tensor(key[:, :, :], key[:, :, :], chosen[:, :, :], ALU.mult))
                    for g in range(TT):
                        ch.done(v.max(key8[:, g, :], key[:, g, :]))
                    ch.settle()
                    ch.done(v.tensor_scalar(key8i[:, :, :], key8[:, :, :], -1.0, None, ALU.add))

                def find_records(b):
                    g = slice(b * RT, (b + 1) * RT)
                    ch.done(v.tensor_copy(record[:, g, :, 0], row_idf[:, g].unsqueeze(2).to_broadcast([P, RT, TOP_EXPERTS])))
                    ch.step(v.tensor_tensor(match[:, :, :, :], key8[:, g, :].unsqueeze(3).to_broadcast([P, RT, TOP_EXPERTS, E]),
                                            key[:, g, :].unsqueeze(2).to_broadcast([P, RT, TOP_EXPERTS, E]), ALU.is_equal))
                    ch.step(v.tensor_tensor(match[:, :, :, :], match[:, :, :, :],
                                            route[:, g, :].unsqueeze(2).to_broadcast([P, RT, TOP_EXPERTS, E]), ALU.mult))
                    ch.step(v.tensor_reduce(record[:, g, :, 1], match[:, :, :, :], AX.X, ALU.add))
                    v.tensor_scalar(record[:, g, :, 1], record[:, g, :, 1], 1.0 / W_SCALE, None, ALU.mult).then_inc(S["records_ready"], 1)

                def count_tiles():
                    dve.wait_ge(S["counts_ready"], 1)
                    ch.step(v.tensor_scalar(n_e[:, :], bank[6][0:E, 0:1], P - 1.0, None, ALU.add))
                    ch.step(v.tensor_copy(n_i[:, :], n_e[:, :]))
                    ch.step(v.tensor_scalar(n_t[:, :], n_i[:, :], 7, None, ALU.arith_shift_right))
                    ch.step(v.tensor_copy(n_e[:, :], n_t[:, :]))
                    v.tensor_scalar(st[:, 1:2], n_e[:, :], 1.0, None, ALU.max).then_inc(S["count_copied"], 1)

                def find_starts():
                    dve.wait_ge(S["starts_ready"], 1)
                    v.tensor_copy(st[:, 0:1], bank[7][0:E, 0:1]).then_inc(S["st_ready"], 1)
                    dve.wait_ge(S["st_ready"], 1)
                    ch.done(v.tensor_scalar(steps[:, 0, :], tile_nof[0:E, :], st[:, 0:1], None, ALU.is_ge))
                    ch.done(v.tensor_scalar(steps[:, 1, :], tile_nof[0:E, :], st[:, 0:1], None, ALU.is_equal))

                def find_slots():
                    dve.wait_ge(S["spread_ready"], 1)
                    ch.step(v.tensor_copy(spread[:, :, :], bank[6][:, 0:2 * QC].rearrange("p (c a) -> p c a", a=2)))
                    ch.done(v.tensor_scalar(live[:, :], spread[:, :, 1], j_off[:, 0:1], None, ALU.is_gt))
                    ch.step(v.tensor_scalar(target[:, :], spread[:, :, 0], j_off[:, 0:1], 1.0, ALU.add, ALU.add))
                    ch.step(v.tensor_tensor(target[:, :], target[:, :], live[:, :], ALU.mult))
                    ch.step(v.tensor_scalar(target[:, :], target[:, :], -1.0, None, ALU.add))
                    for c in range(QC):
                        t = v.tensor_scalar(onehot[:, c, :], tile_nof[:, :], target[:, c:c + 1], None, ALU.is_equal)
                        if c < QC - 1:
                            ch.done(t)
                    t.then_inc(S["onehot_ready"], 1)


                between = {0: [find_keys], 1: [lambda: find_records(0)], 2: [lambda: find_records(1), count_tiles],
                           3: [lambda: find_records(2), find_starts], 4: [lambda: find_records(3)], 5: [find_slots]}
                convert(0)
                for h in range(SH):
                    for n in range(0, OPEN[h]):
                        shared(h * TT + n, (n - 1) % TT if h or n else None, n % 2)
                        if h == 0:
                            for part in between[n]:
                                part()
                    convert(h + 1)
                    with dve.Fori(OPEN[h], TT - 1, 2) as g:
                        for s in range(2):
                            shared(g + (s + h * TT), g + (s - 1), s)
                add_shared(SN - 1, TT - 1, 1)
                dve.wait_ge(S["ids_psum"], 1)
                ch.step(v.tensor_copy(ids[:, :], bank[6][:, 0:NT]))
                ch.done(v.tensor_copy(wts[:, :], bank[6][:, NT:2 * NT]))
                ch.step(v.tensor_scalar(pad[:, :], ids[:, :], 0.0, trashf[:, 0:1], ALU.is_le, ALU.mult))
                ch.step(v.scalar_tensor_tensor(ids[:, :], ids[:, :], -1.0, pad[:, :], ALU.add, ALU.add))
                ch.done(v.tensor_copy(ids_i[:, :], ids[:, :]))
                ch.done(v.tensor_scalar(tile_info[0:1, 0, :], bank[7][0:1, 0:NT], -1.0, None, ALU.add))
                ch.step(v.tensor_copy(in_use[:, :], bank[7][0:1, 2 * NT:2 * NT + 1]))
                ch.done(v.tensor_scalar(tile_info[0:1, 2, :], tile_nof[0:1, :], in_use[0:1, 0:1], None, ALU.is_le))
                ch.step(v.tensor_scalar(results[:, :], in_use[:, :], PLAIN - 1.0, None, ALU.max))
                v.tensor_copy(tile_info[0:1, 1, :], bank[7][0:1, NT:2 * NT]).then_inc(S["tables_ready"], 1)

                def split_rows(t, s):
                    dve.wait_ge(S["xg_hi"], t + 1)
                    v.tensor_tensor(xgT[:, s, 1, :, :], bank[XB[s]][:, :].rearrange("p (k t) -> p k t", k=KC), xgT[:, s, 0, :, :],
                                    ALU.subtract).then_inc(S["xg_lo"], 1)

                def gates(t, s):
                    dve.wait_ge(S["b_silu"], t + 1)
                    if not (isinstance(t, int) and t < 2):
                        dve.wait_ge(S["b_hidT"], t - 1)
                    v.scalar_tensor_tensor(hid[:, s, :], bank[GU[s]][:, I:2 * I], 1.0 / W_SCALE, silu[:, s, :],
                                           ALU.mult, ALU.mult).then_inc(S["b_hid"], 1)

                def next_weights(t):
                    with dve.If(info_of(dve, 1, t) > 0):
                        convert(info_of(dve, 0, t) + (SH + 1))

                def hidden(t, s):
                    dve.wait_ge(S["b_hhi"], t + 1)
                    v.tensor_tensor(hT16[:, s, 1, :], bank[HT[s]][:, 0:I], hT16[:, s, 0, :], ALU.subtract).then_inc(S["b_hlo"], 1)

                dve.wait_ge(S["tables_ready"], 1)
                split_rows(0, 0)
                split_rows(1, 1)
                for t in range(2):
                    gates(t, t)
                    split_rows(t + 2, t)
                    next_weights(t)
                    hidden(t, t)
                def step(t, s):
                    gates(t, s)
                    split_rows(t + 2, s)
                    next_weights(t)
                    hidden(t, s)

                with dve.Fori(2, PLAIN - 1, 2) as t:
                    for s in range(2):
                        step(t + s, s)
                with dve.Fori(PLAIN, PLAIN + E - SKIP + 1, SKIP) as t:
                    with dve.If(info_of(dve, 2, t) > 0):
                        for i in range(SKIP):
                            with dve.If(info_of(dve, 2, t + i) > 0):
                                step(t + i, i % 2)

            @block.tensor
            def _(pe):
                flat = chosen[:, :, :].rearrange("p g e -> p (g e)")
                nc.tensor.matmul(bank[6][:, :], before[:, :], flat, start=True, stop=True).then_inc(S["cum_ready"], 1)
                nc.tensor.matmul(bank[7][:, :], ones[:, :], flat, start=True, stop=True).then_inc(S["cum_ready"], 1)

                def count_tokens():
                    pe.wait_ge(S["records_ready"], 1)
                    for g in range(TT):
                        t = nc.tensor.matmul(bank[6][0:E, 0:1], chosen[:, g, :], ones[:, 0:1], start=(g == 0), stop=(g == TT - 1))
                    t.then_inc(S["counts_ready"], 1)

                def sum_starts():
                    pe.wait_ge(S["count_copied"], 1)
                    nc.tensor.matmul(bank[7][0:E, 0:1], before[0:E, 0:E], st[:, 1:2], start=True, stop=True).then_inc(S["starts_ready"], 1)

                def spread_starts():
                    pe.wait_ge(S["st_ready"], 1)
                    for c in range(QC):
                        t = nc.tensor.matmul(bank[6][:, 2 * c:2 * c + 2], expand[:, c * P:(c + 1) * P], st[:, :], start=True, stop=True)
                    t.then_inc(S["spread_ready"], 1)

                def gate_up(cols, s, ws):
                    return three(bank[GU[s]][:, :], lambda a, c: xT16[:, a, c, cols], lambda w, c: gu16[:, ws, w, c, :], KC)

                def transposes(s):
                    for c in range(IC):
                        t = nc.tensor.transpose(bank[HT[s]][:, c * P:(c + 1) * P], hid[:, s, c * P:(c + 1) * P], ident[:, :])
                    return t

                def s_transposes(n, s):
                    pe.wait_ge(S["hid_ready"], n + 1)
                    transposes(s).then_inc(S["hidT_ready"], 1)

                def s_down(n, s, ws):
                    pe.wait_ge(S["hlo_ready"], n + 1)
                    three(bank[DN[s]][:, :], lambda a, c: hT16[:, s, a, c * P:(c + 1) * P], lambda w, c: dn16[:, ws, w, c, :], IC).then_inc(S["down_ready"], 1)

                def s_tile(n, cols, s, h, prev):
                    if not (isinstance(n, int) and n < 2):
                        pe.wait_ge(S["hid_ready"], n - 1)
                    gate_up(cols, s, h % 2).then_inc(S["gu_ready"], 1)
                    if not (isinstance(n, int) and n < 1):
                        if not (isinstance(n, int) and n < 3):
                            pe.wait_ge(S["added"], n - 2)
                        s_down(n - 1, 1 - s, prev % DS)
                    s_transposes(n, s)

                between = {2: count_tokens, 3: sum_starts, 4: spread_starts}
                for h in range(SH):
                    pe.wait_ge(S["b_wlo"], PIECES * (h + 1))
                    for i in range(OPEN[h]):
                        s_tile(h * TT + i, slice(i * P, (i + 1) * P), i % 2, h, h if i else h - 1)
                        if h == 0 and i in between:
                            between[i]()
                    with pe.Fori(OPEN[h], TT - 1, 2) as g:
                        for s in range(2):
                            s_tile(g + (h * TT + s), bass.ds((g + s) * P, P), s, h, h)
                s_down(SN - 1, 1, SH - 1)

                pe.wait_ge(S["onehot_ready"], 1)
                pe.wait_ge(S["table_loaded"], 16)
                for a in range(2):
                    for c in range(QC):
                        nc.tensor.matmul(bank[6][:, a * NT:(a + 1) * NT], tab[:, c, :, a], onehot[:, c, :], start=(c == 0), stop=(c == QC - 1))
                nc.tensor.matmul(bank[7][0:1, 0:NT], ones[0:E, 0:1], steps[:, 0, :], start=True, stop=True)
                nc.tensor.matmul(bank[7][0:1, NT:2 * NT], ones[0:E - 1, 0:1], steps[0:E - 1, 1, :], start=True, stop=True)
                t = nc.tensor.matmul(bank[7][0:1, 2 * NT:2 * NT + 1], ones[0:E, 0:1], st[:, 1:2], start=True, stop=True)
                t.then_inc(S["ids_psum"], 1)
                pe.wait_ge(S["tables_ready"], 1)
                pe.wait_ge(S["hhi_ready"], SN)

                def rows_T(t, s, x):
                    pe.wait_ge(S[f"gathered{x}"], (t - x) * (16 // XG) + 16)
                    if not (isinstance(t, int) and t < 2):
                        pe.wait_ge(S["xg_lo"], t - 1)
                    for c in range(KC):
                        last = nc.tensor.transpose(bank[XB[s]][:, c * P:(c + 1) * P], xg[:, x, c * P:(c + 1) * P], ident[:, :])
                    last.then_inc(S["xgT_ready"], 1)

                def gate_up_of(t, s):
                    e = info_of(pe, 0, t)
                    pe.wait_ge(S["b_wlo"], PIECES * e + (SH + 1) * PIECES)
                    pe.wait_ge(S["xg_lo"], t + 1)
                    if not (isinstance(t, int) and t < 2):
                        pe.wait_ge(S["b_hid"], t - 1)
                    w_slot = (e + SH) % 2
                    three(bank[GU[s]][:, :], lambda a, c: xgT[:, s, a, c, :],
                          lambda w, c: gu16[:, bass.ds(w_slot, 1), w, c, :].rearrange("p a n -> p (a n)"), KC).then_inc(S["b_gu"], 1)

                def hidden_T(t, s):
                    pe.wait_ge(S["b_hid"], t + 1)
                    if not (isinstance(t, int) and t < 2):
                        pe.wait_ge(S["b_hlo"], t - 1)
                    transposes(s).then_inc(S["b_hidT"], 1)

                def down_of(t, s):
                    w_slot = (info_of(pe, 0, t) + SH) % DS
                    pe.wait_ge(S["b_hlo"], t + 1)
                    if not (isinstance(t, int) and t < 2):
                        pe.wait_ge(S["y_ready"], t - 1)
                    three(bank[DN[s]][:, :], lambda a, c: hT16[:, s, a, c * P:(c + 1) * P],
                          lambda w, c: dn16[:, bass.ds(w_slot, 1), w, c, :].rearrange("p a n -> p (a n)"), IC).then_inc(S["b_down"], 1)

                rows_T(0, 0, 0)
                rows_T(1, 1, 1)
                gate_up_of(0, 0)
                for t in range(2):
                    rows_T(t + 2, t, t + 2)
                    gate_up_of(t + 1, 1 - t)
                    hidden_T(t, t)
                    if t:
                        down_of(t - 1, 1 - t)
                def step(t, i):
                    s = i % 2
                    rows_T(t + 2, s, i)
                    gate_up_of(t + 1, 1 - s)
                    hidden_T(t, s)
                    down_of(t - 1, 1 - s)

                with pe.Fori(2, PLAIN - 3, 4) as t:
                    for i in range(4):
                        step(t + i, i)
                with pe.Fori(PLAIN, PLAIN + E - SKIP + 1, SKIP) as t:
                    with pe.If(info_of(pe, 2, t) > 0):
                        for i in range(SKIP):
                            with pe.If(info_of(pe, 2, t + i) > 0):
                                step(t + i, i % 4)


_INS = ["x", "ctx_512", "L0_xattn_Wq", "L0_xattn_Wk", "L0_xattn_gamma_raw", "L0_ffn_router_w", "L0_ffn_router_bias",
        "L0_ffn_w_gate", "L0_ffn_w_up", "L0_ffn_w_down", "L0_ffn_sw_gate", "L0_ffn_sw_up", "L0_ffn_sw_down"]
_OUTS = [((4 * 512 + 128, 512), "float32")]


def kernel(**inputs):
    import numpy as _np
    import concourse.bacc as _bacc
    from concourse import mybir as _mybir
    from concourse.bass_utils import run_bass_kernel_spmd as _run

    nc = _bacc.Bacc("TRN2", target_bir_lowering=False, num_devices=1)
    arrays, args = {}, []
    for name in _INS:
        a = _np.ascontiguousarray(inputs[name])
        a = a.reshape(a.shape or (1,))
        arrays[f"in_{name}_dram"] = a
        args.append(nc.dram_tensor(f"in_{name}_dram", a.shape, _mybir.dt.from_np(a.dtype), kind="ExternalInput").ap())
    for i, (shape, dtype) in enumerate(_OUTS):
        dt = _mybir.dt.from_np(_np.dtype(dtype))
        args.append(nc.dram_tensor(f"out_{i}_dram", shape, dt, kind="ExternalOutput").ap())
    xattn_moe_kernel(nc, *args)
    r = _run(nc, [arrays], core_ids=[0])
    return _np.asarray(r.results[0]["out_0_dram"])[:4 * 512].reshape(4, 512, 512)
```
